# Optimizing a Trainium2 kernel written in Bass

```python
import numpy as np
import jax
import jax.numpy as jnp

def _softmax(x, axis=-1):
    return jax.nn.softmax(x, axis=axis)

def _gelu(x):
    return jax.nn.gelu(x, approximate=True)

def _silu(x):
    return jax.nn.silu(x)

def _sigmoid(x):
    return jax.nn.sigmoid(x)

def _layernorm(x, axis=-1, eps=1e-05):
    m = jnp.mean(x, axis=axis, keepdims=True)
    v = jnp.var(x, axis=axis, keepdims=True)
    return (x - m) / jnp.sqrt(v + eps)

def _scatter_add(tgt, idx, src, axis=0):
    return tgt.at[idx].add(src)

def _segment_sum(src, seg, n):
    return jax.ops.segment_sum(src, seg, n)
kernel_name = 'mk_macaron_d1_jaxref_r4_37a46c'

def setup_inputs(seed: int=0):
    np.random.seed(seed)
    _w = jnp.asarray

    def _L0_attn_setup():
        import jax, jax.numpy as jnp
        import numpy as np
        H = 16

        def _split_heads(t):
            B, N, D = t.shape
            return t.reshape(B, N, H, D // H).transpose(0, 2, 1, 3)
        key = jax.random.key(seed)
        ks = jax.random.split(key, 9)
        B, N, D = (4, 1024, 256)
        mk = lambda k, shape: jax.random.normal(k, shape, dtype=jnp.float32) * 0.02
        return {'x': jax.random.normal(ks[0], (B, N, D), dtype=jnp.float32), 'Wq': mk(ks[1], (D, D)), 'bq': mk(ks[2], (D,)), 'Wk': mk(ks[3], (D, D)), 'bk': mk(ks[4], (D,)), 'Wv': mk(ks[5], (D, D)), 'bv': mk(ks[6], (D,)), 'Wo': mk(ks[7], (D, D)), 'bo': mk(ks[8], (D,))}
    _L0_attn_in = _L0_attn_setup()

    def _L0_ffn_setup():
        import jax, jax.numpy as jnp
        import numpy as np
        E = 8
        K = 2
        CF = 1.25
        key = jax.random.key(seed)
        kx, kr, kg, ku, kd = jax.random.split(key, 5)
        D, F = (256, 1024)
        x = jax.random.normal(kx, (4, 512, D), dtype=jnp.float32)
        router_w = 0.02 * jax.random.normal(kr, (E, D), dtype=jnp.float32)
        wg = jax.random.normal(kg, (E, D, F), dtype=jnp.float32) / np.sqrt(D)
        wu = jax.random.normal(ku, (E, D, F), dtype=jnp.float32) / np.sqrt(D)
        wd = jax.random.normal(kd, (E, F, D), dtype=jnp.float32) / np.sqrt(F)
        return {'x': x, 'router_w': router_w, 'wg': wg, 'wu': wu, 'wd': wd}
    _L0_ffn_in = _L0_ffn_setup()
    _d = {'L0_attn_x': _L0_attn_in['x'], 'L0_attn_Wq': _L0_attn_in['Wq'], 'L0_attn_bq': _L0_attn_in['bq'], 'L0_attn_Wk': _L0_attn_in['Wk'], 'L0_attn_bk': _L0_attn_in['bk'], 'L0_attn_Wv': _L0_attn_in['Wv'], 'L0_attn_bv': _L0_attn_in['bv'], 'L0_attn_Wo': _L0_attn_in['Wo'], 'L0_attn_bo': _L0_attn_in['bo'], 'L0_ffn_router_w': _L0_ffn_in['router_w'], 'L0_ffn_wg': _L0_ffn_in['wg'], 'L0_ffn_wu': _L0_ffn_in['wu'], 'L0_ffn_wd': _L0_ffn_in['wd']}
    _x0 = _d['L0_attn_x']
    _d['L0_attn_x'] = jax.random.normal(jax.random.fold_in(jax.random.key(seed), 1), (4, 2048, 256), dtype=_x0.dtype)
    del _x0
    return _d

def reference(L0_attn_x, L0_attn_Wq, L0_attn_bq, L0_attn_Wk, L0_attn_bk, L0_attn_Wv, L0_attn_bv, L0_attn_Wo, L0_attn_bo, L0_ffn_router_w, L0_ffn_wg, L0_ffn_wu, L0_ffn_wd):

    def _L0_attn_ref(x, Wq, bq, Wk, bk, Wv, bv, Wo, bo):
        import jax, jax.numpy as jnp
        import numpy as np
        H = 16

        def _split_heads(t):
            B, N, D = t.shape
            return t.reshape(B, N, H, D // H).transpose(0, 2, 1, 3)
        B, N, D = x.shape
        d_head = D // H
        s = (d_head ** 0.5) ** (-0.25)
        q = _split_heads(x @ Wq + bq)
        _ = x @ Wk + bk
        v = _split_heads(x @ Wv + bv)
        q = jax.nn.softmax(q, axis=-1) * s
        k = jax.nn.softmax(q, axis=-2) * s
        ctx = jnp.einsum('bhnd,bhne->bhde', k, v)
        attn = jnp.einsum('bhnd,bhde->bhne', q, ctx)
        attn = attn.transpose(0, 2, 1, 3).reshape(B, N, D)
        return attn @ Wo + bo

    def _L0_ffn_ref(x, router_w, wg, wu, wd):
        import jax, jax.numpy as jnp
        import numpy as np
        E = 8
        K = 2
        CF = 1.25
        B, L, D = x.shape
        xf = x.reshape(-1, D)
        N = xf.shape[0]
        capacity = max(1, int(CF * N / E))
        logits = xf @ router_w.T
        probs = jax.nn.softmax(logits, axis=-1)
        topw, topi = jax.lax.top_k(probs, K)
        topw = topw / (topw.sum(-1, keepdims=True) + 1e-06)
        fe = topi.reshape(-1)
        fw = topw.reshape(-1)
        ft = jnp.repeat(jnp.arange(N), K)
        order = jnp.lexsort((-fw, fe))
        se, sw, st = (fe[order], fw[order], ft[order])
        counts = jax.ops.segment_sum(jnp.ones_like(se), se, num_segments=E)
        starts = jnp.cumsum(counts) - counts
        rank = jnp.arange(N * K) - starts[se]
        keep = rank < capacity
        pos = jnp.where(keep, rank, capacity)
        disp = jnp.zeros((E, capacity + 1, D), x.dtype).at[se, pos].set(xf[st])
        disp = disp[:, :capacity]
        g = jnp.einsum('ecd,edf->ecf', disp, wg)
        u = jnp.einsum('ecd,edf->ecf', disp, wu)
        eo = jnp.einsum('ecf,efd->ecd', jax.nn.silu(g) * u, wd)
        gathered = eo[se, jnp.minimum(pos, capacity - 1)]
        contrib = gathered * (sw * keep.astype(x.dtype))[:, None]
        out = jnp.zeros_like(xf).at[st].add(contrib)
        return out.reshape(B, L, D)
    x = L0_attn_x
    x = x + 0.5 * _L0_ffn_ref(_layernorm(x, axis=-1), L0_ffn_router_w, L0_ffn_wg, L0_ffn_wu, L0_ffn_wd)
    x = x + _L0_attn_ref(_layernorm(x, axis=-1), L0_attn_Wq, L0_attn_bq, L0_attn_Wk, L0_attn_bk, L0_attn_Wv, L0_attn_bv, L0_attn_Wo, L0_attn_bo)
    x = x + 0.5 * _L0_ffn_ref(_layernorm(x, axis=-1), L0_ffn_router_w, L0_ffn_wg, L0_ffn_wu, L0_ffn_wd)
    return x

_drawn_inputs = setup_inputs


def setup_inputs(seed=0):
    import zlib

    import numpy as np

    out = dict(_drawn_inputs(seed))
    spreads = {}
    factors = {'L0_attn_Wq': 26.057,
     'L0_attn_bq': 200.0,
     'L0_attn_Wv': 8.0,
     'L0_attn_bv': 5.917,
     'L0_attn_Wo': 6.276}
    for name, (base, spread) in spreads.items():
        noise = np.random.default_rng([zlib.crc32(name.encode()), seed]).standard_normal(out[name].shape)
        drawn = base * np.exp(spread * noise) if base else spread * noise
        out[name] = jnp.asarray(drawn.astype(out[name].dtype))
    for name, factor in factors.items():
        out[name] = (out[name] * factor).astype(out[name].dtype)
    return out
```

```python
import concourse.bass as bass
from concourse import mybir
from contextlib import ExitStack
from collections import namedtuple


def macaron_block(nc, x, wq, bq, wv, bv, wo, bo, router_w, wg, wu, wd, out):
    f32, f16, b16, i32, u32 = (mybir.dt.float32, mybir.dt.float16, mybir.dt.bfloat16,
                               mybir.dt.int32, mybir.dt.uint32)
    ALU, ACT, AX = mybir.AluOpType, mybir.ActivationFunctionType, mybir.AxisListType
    add, sub, mult = ALU.add, ALU.subtract, ALU.mult

    P = 128
    B, SEQ, D = x.shape
    N = B * SEQ
    E, _, F = wg.shape
    TOPK = 2
    C = int(1.25 * N / E)
    NT = N // P
    KD = D // P
    FT = F // P
    H = 16
    DH = D // H
    HS = float((DH ** 0.5) ** -0.25)
    QTOP = 2.0 ** 14
    BT = SEQ // P
    QUADS = BT // 4
    ST = C // P
    CH = 4
    CW = C // CH
    HB = 4
    UNITS = FT * CH
    G4 = 4
    PAIR = 2 * G4
    STEPS = NT // PAIR
    TC = NT // G4
    LT = 8
    LP = NT // LT
    EPS = 1e-5
    XSCALE = 2.0 ** 10
    WTOP = 13
    EXPERT_STEPS = 19
    LOOP_STEPS = 52
    HSHIFT = 2.0 ** -39
    ONE = 1 << 23

    xf = x.rearrange("b n d -> (b n) d")
    of = out.rearrange("b n d -> (b n) d")
    x_v = xf.rearrange("(t p) d -> p t d", p=P)
    o_v = of.rearrange("(t p) d -> p t d", p=P)

    ctx = ExitStack()
    with ctx:
        def sb(name, shape, dt):
            return ctx.enter_context(nc.sbuf_tensor(name, shape, dt))

        def sem(name):
            return ctx.enter_context(nc.semaphore(name))

        bank = [ctx.enter_context(nc.psum_tensor(f"bank{i}", [P, 512], f32)) for i in range(8)]

        rows_d = nc.dram_tensor("rows_d", [N, 2 * D], f16, kind="Internal").ap()
        x1_d = nc.dram_tensor("x1_d", [N, D], f32, kind="Internal").ap()
        rows_v = rows_d.rearrange("(t p) c -> p t c", p=P)
        x1_v = x1_d.rearrange("(t p) d -> p t d", p=P)

        xs = sb("xs", [P, NT, D], f32)
        flat = xs[:, :, :].rearrange("p t d -> p (t d)")
        hcols = FT * C
        hid = flat[:, 0:hcols].bitcast(f16).rearrange("p (a f c) -> p a f c", a=2, f=FT)
        stage = flat[:, hcols:hcols + ST * D].rearrange("p (s d) -> p s d", s=ST)
        rows = sb("rows", [P, 2, G4, 2 * D], f16)
        xn = sb("xn", [P, 2, G4, D], f32)
        xt2 = sb("xt2", [P, 2, 2, 2 * KD, P], f16)
        bst = sb("bst", [P, 2, G4, 6], f32)
        mv = sb("mv", [P, 2, G4, 2], f32)
        rstd = sb("rstd", [P, 2, G4], f32)
        ident16 = sb("ident16", [P, P], f16)
        ident = sb("ident", [P, P], f32)
        sel8 = sb("sel8", [P, E], f32)
        same_e = sb("same_e", [P, P], f32)
        before_e = sb("before_e", [P, P], f32)
        edesc = sb("edesc", [P, E], f32)
        mhalf = sb("mhalf", [P, G4], f32)
        slot_a = sb("slot_a", [P, P, LT], b16)
        slot_b = sb("slot_b", [P, ST], f32)
        bit_f = sb("bit_f", [P, 32], f32)
        bit_i = sb("bit_i", [P, 32], i32)
        pid = sb("pid", [P, 1], f32)
        rw8 = sb("rw8", [E, D], f32)
        rwa = sb("rwa", [P, 2], f32)
        rws = sb("rws", [P, 8], f32)
        rwh = sb("rwh", [E, 2, D], f16)
        rwT = sb("rwT", [P, 2, KD, E], f16)
        lg = sb("lg", [P, NT, E], f32)
        t1 = sb("t1", [P, NT, E], f32)
        t2 = sb("t2", [P, NT, E], f32)
        t3 = sb("t3", [P, NT, E], f32)
        v1 = sb("v1", [P, NT], f32)
        v2 = sb("v2", [P, NT], f32)
        wT = sb("wT", [P, 4 * P], f32)
        kT = sb("kT", [P, 4 * P], f32)
        rT = sb("rT", [P, 4 * P], f32)
        cand = sb("cand", [P, 1], i32)
        flip = sb("flip", [P, 1], i32)
        cnt = sb("cnt", [P, 2], f32)
        tot = sb("tot", [P, 4], f32)
        pos_a = sb("pos_a", [P, E, NT], b16)
        pos_b = sb("pos_b", [P, E, NT], b16)
        val = sb("val", [P, E, NT, 5], b16)
        hot_a = sb("hot_a", [P, 2, P, LT], b16)
        hot_b = sb("hot_b", [P, 2, LT, ST], b16)
        hot_v = sb("hot_v", [P, 2, LT, 5, ST], b16)
        id_next = sb("id_next", [P, ST], u32)
        id_cur = sb("id_cur", [P, ST], u32)
        w_next = sb("w_next", [P, ST], f32)
        w_tmp = sb("w_tmp", [P, ST], f32)
        w_fac = sb("w_fac", [P, ST], f32)
        lst = sb("lst", [P, 5 * ST], f32)
        spare_v = sb("spare_v", [P, 1], f32)
        v3 = sb("v3", [P, NT], f32)
        raw_gu = sb("raw_gu", [P, 2, KD * F], f32)
        raw_d = sb("raw_d", [P, KD * F], f32)
        raw = [raw_gu[:, 0, :], raw_gu[:, 1, :], raw_d[:, :]]
        wgu = [sb(f"w16_{m}", [P, 2, KD, F], f16) for m in "gu"]
        wdn = sb("w16_d", [P, 2, FT, D], f16)
        am = sb("am", [P, 3], f32)
        amr = sb("amr", [P, 3], f32)
        sc_next = sb("sc_next", [P, 6], f32)
        sc_cur = sb("sc_cur", [P, 6], f32)
        gat = sb("gat", [P, ST, 2 * D], f16)
        xT = sb("xT", [P, 2 * KD, C], f16)
        unit_buf = sb("unit_buf", [P, G4 * 2 * D], f32)
        act_s = unit_buf[:, 0:2 * CW].rearrange("p (b c) -> p b c", b=2)
        h32 = unit_buf[:, 2 * CW:(2 + HB) * CW].rearrange("p (b c) -> p b c", b=HB)
        wq32 = sb("wq32", [P, KD, D], f32)
        wv32 = sb("wv32", [P, KD, D], f32)
        wo32 = sb("wo32", [P, KD, D], f32)
        wq16 = sb("wq16", [P, 2, KD, D], f16)
        bq_b = sb("bq_b", [P, D], f32)
        bo_b = sb("bo_b", [P, D], f32)
        bv_p = sb("bv_p", [P, KD], f32)
        same_h = sb("same_h", [P, P], f32)
        mbv = sb("mbv", [P, KD, P], f32)
        sel_h = sb("sel_h", [P, P // DH], f32)
        ones = sb("ones", [P, 1], f16)
        qb = gat[:, :, :].rearrange("p s c -> p (s c)")[:, 0:4 * G4 * D].bitcast(f32).rearrange(
            "p (b t d) -> p b t d", b=2, t=G4)
        ekb = xT[:, :, :].rearrange("p k c -> p (k c)")[:, 0:4 * G4 * D].bitcast(f32).rearrange(
            "p (b t d) -> p b t d", b=2, t=G4)
        qrow = unit_buf[:, :].bitcast(f16).rearrange("p (b t c) -> p b t c", b=2, t=G4)
        ekrow = wdn[:, :, :, :].rearrange("p a f d -> p (a f d)").rearrange("p (b t c) -> p b t c", b=2, t=G4)
        qT = raw_gu[:, :, :].rearrange("p m c -> p (m c)").bitcast(f16).rearrange(
            "p (t c n) -> p t c n", t=BT, c=2 * KD)
        qmax = sb("qmax", [P, G4 * H], f32)
        gt_s = t2[:, :, :].rearrange("p t e -> p (t e)").rearrange("p (k d) -> p k d", k=KD)
        m2f = t3[:, :, :].rearrange("p t e -> p (t e)").rearrange("p (k d) -> p k d", k=KD)
        bvo = rT[:, :].rearrange("p (k d) -> p k d", k=KD)
        ctm = wT[:, 0:KD * P].rearrange("p (k d) -> p k d", k=KD)
        m2h = kT[:, :].bitcast(f16).rearrange("p (a k d) -> p a k d", a=2, k=KD)
        zr = sb("zr", [P, KD], f32)
        mx2 = sb("mx2", [P, 5], f32)

        s_const = sem("constants_ready")
        s_rwld = sem("router_loaded")
        s_boot = sem("boot_steps_dve")
        s_bootp = sem("boot_steps_pool")
        s_boota = sem("boot_steps_act")
        s_bootpe = sem("boot_steps_pe")
        s_gstep = sem("pool_const_steps")
        s_bootx = sem("boot_scale_steps")
        s_passed = sem("waits_passed")
        s_atw = sem("attention_loaded")

        def ffn_sems(p):
            names = ("loaded kept stat_ready rstd_ready xn_ready hi_ready lo_ready stored turned turned_ok cent_ready "
                     "logit_ready logit_out dstep ex_ready w_ready wt_turned counted compared ranked offset_ready "
                     "slots_ready back_turned piece_ready piece_used ids_ready "
                     "raw_g raw_u raw_d amax_ready amax_all scales_ready gu_hi gu_lo d_hi d_lo cur_ready "
                     "g_ready u_ready s_ready h32_ready hhi_ready h_ready d_ready d_out landed added "
                     "xt_turned xt_ready wfac_ready").split()
            first = E * "ab".index(p)
            return namedtuple("FfnSems", names + ["first"])(*(sem(f"{n}_{p}") for n in names), first)

        class Chain:

            def __init__(self, eng, sm):
                self.eng, self.sm, self.base, self.n = eng, sm, 0, 0

            def mark(self, ins):
                self.n += 1
                return ins.then_inc(self.sm, 1)

            def wait(self):
                self.eng.wait_ge(self.sm, self.base + self.n)

            def step(self, ins):
                self.mark(ins)
                self.wait()

            def enter(self, i, per):
                self.start, self.per = self.base + self.n, per
                self.base, self.n = self.start + i * per, 0

            def leave(self, trips):
                assert self.n == self.per, (self.n, self.per)
                self.base, self.n = self.start + trips * self.per, 0

        gathered = [sem(f"gathered{j}") for j in range(ST // 2)]
        sems = [ffn_sems("a"), ffn_sems("b")]
        at_names = ("x1_in stat rstd xn hi lo xt_turned xt q qout cent ex qs qhi qlo ekhi eklo gt gt_out qt_turned qt "
                    "out x2 bo ctx ctm a m_amax m_max m_scale m_hi m_lo dstep").split()
        at = namedtuple("AttentionSems", at_names)(*(sem(f"at_{n}") for n in at_names))
        block = ctx.enter_context(nc.Block())
        bank16 = [b[:, :].bitcast(f16) for b in bank]

        def settle(eng):
            eng.sem_inc(s_passed, 1)

        def scales(ch, v, a, s, inv):
            ch.step(v.tensor_scalar_max(s, a, 2.0 ** -20))
            ch.step(v.tensor_scalar(s.bitcast(i32), s.bitcast(i32), 0x7F800000, None, ALU.bitwise_and))
            ch.step(v.tensor_scalar(s.bitcast(i32), s.bitcast(i32), -1.0, float((254 + WTOP) * ONE), mult, add))
            ch.step(v.tensor_scalar(inv.bitcast(i32), s.bitcast(i32), -1.0, float(254 * ONE), mult, add))

        def raw_src(n):
            pick = (lambda w: w[n:n + 1, :, :]) if isinstance(n, int) else (lambda w: w[bass.ds(n, 1), :, :])
            return [pick(wg).rearrange("o (k p) f -> p (o k) f", p=P),
                    pick(wu).rearrange("o (k p) f -> p (o k) f", p=P),
                    pick(wd).rearrange("o (j p) d -> p (o j) d", p=P)]

        raw_dst = [raw[0].rearrange("p (k f) -> p k f", k=KD),
                   raw[1].rearrange("p (k f) -> p k f", k=KD),
                   raw[2].rearrange("p (j d) -> p j d", j=FT)]

        def halves(m, h):
            if m < 2:
                r = raw_dst[m][:, :, h * F // 2:(h + 1) * F // 2]
                w = wgu[m][:, :, :, h * F // 2:(h + 1) * F // 2]
            else:
                r = raw_dst[2][:, h * FT // 2:(h + 1) * FT // 2, :]
                w = wdn[:, :, h * FT // 2:(h + 1) * FT // 2, :]
            return r, w[:, 0], w[:, 1]

        RMAX = bass.bass_isa.ReduceOp.max

        def bc(ap, axis, n):
            ap = ap.unsqueeze(axis)
            shape = list(ap.shape)
            shape[axis] = n
            return ap.to_broadcast(shape)

        def col(ap, i, n=1):
            return ap[:, i:i + n] if isinstance(i, int) else ap[:, bass.ds(i, n)]

        def wait_for(eng, sm, n):
            if not (isinstance(n, int) and n <= 0):
                eng.wait_ge(sm, n)

        def tiles(ap, t, n):
            return ap[:, t:t + n] if isinstance(t, int) else ap[:, bass.ds(t, n)]

        def batches(eng, body):
            body(0, True, False)
            with eng.Fori(0, B - 2) as i:
                body(i + 1, False, False)
            body(B - 1, False, False)
            body(B, False, True)

        def next_quad(b, j):
            return (b, j + 1) if j + 1 < QUADS else (b + 1, 0)

        FINISH = {0: (), 1: (0,), 2: (1,), 3: (2, 3)}
        lg_gt = lg[:, :, :].rearrange("p (g t) e -> p g t e", g=G4)
        xt2_flat = xt2[:, :, :, :, :].rearrange("p h t c n -> p h (t c n)")
        PIECE_AT = {6 + 2 * i: i for i in range(LP)}
        PE_PIECE_AT = {u + 3: i for u, i in PIECE_AT.items()}
        XT_AT = 4

        @block.gpsimd
        def _(pool):
            gs = Chain(pool, s_gstep)
            gs.mark(pool.memset(ident[:, :], 0.0))
            gs.step(pool.memset(ident16[:, :], 0.0))
            for m in (ident, ident16):
                gs.mark(pool.affine_select(out=m[:, :], in_=m[:, :], compare_op=ALU.not_equal, fill=1.0, base=0,
                                           pattern=[[-1, P]], channel_multiplier=1))
            small = dict(allow_small_or_imprecise_dtypes=True)
            gs.mark(pool.iota(edesc[:, :], [[-1, E]], base=E, channel_multiplier=0, **small))
            gs.mark(pool.iota(slot_a[:, :, :], [[1, P], [0, LT]], base=0, channel_multiplier=0, **small))
            gs.mark(pool.iota(slot_b[:, :], [[1, ST]], base=1, channel_multiplier=0, **small))
            gs.mark(pool.iota(val[:, :, :, 0].rearrange("p e (g t) -> p e g t", g=G4),
                              [[0, E], [1, G4], [G4, TC]], base=0, channel_multiplier=0, **small))
            gs.mark(pool.iota(val[:, :, :, 1], [[0, E], [0, NT]], base=0, channel_multiplier=1, **small))
            gs.mark(pool.memset(mhalf[:, :], -0.5))
            for b in range(31):
                gs.mark(pool.memset(bit_f[:, b:b + 1], float(1 << (30 - b))))
            gs.step(pool.memset(bit_f[:, 31:32], 0.0))
            gs.mark(pool.tensor_copy(bit_i[:, :], bit_f[:, :]))
            for S in sems:
                for sm, n in ((S.stored, 32), (S.turned_ok, 2), (S.logit_out, 1), (S.s_ready, 2), (S.h32_ready, 2),
                              (S.h_ready, HB), (S.d_out, 2), (S.d_ready, 1), (S.xt_ready, 1), (S.piece_used, 2)):
                    pool.sem_inc(sm, n)
            pool.wait_ge(s_boot, 2)
            gs.step(pool.affine_select(out=before_e[:, :], in_=same_e[:, :], compare_op=ALU.is_gt, fill=0.0, base=0,
                                       pattern=[[1, P]], channel_multiplier=-1))
            pool.sem_inc(s_const, 1)
            pool.wait_ge(s_boot, 4)
            pool.partition_all_reduce(rws[:, 4:6], rwa[:, :], P, RMAX).then_inc(s_bootp, 1)

            def weight_max(S, n):
                pool.wait_ge(S.amax_ready, 3 * n + 3)
                settle(pool)
                pool.partition_all_reduce(amr[:, :], am[:, :], P, RMAX).then_inc(S.amax_all, 1)

            def gather(S, n):
                pool.wait_ge(S.ids_ready, n + 1)
                settle(pool)
                for s in range(ST):
                    pool.indirect_dma_start(
                        out=gat[:, s, :], out_offset=None, in_=rows_d,
                        in_offset=bass.IndirectOffsetOnAxis(ap=id_next[:, s:s + 1], axis=0),
                        bounds_check=N - 1).then_inc(gathered[s // 2], 16)

            def expert(S, e, dst, last):
                if not last:
                    weight_max(S, e + 1)
                    gather(S, e + 1)
                for s in range(ST):
                    pool.wait_ge(S.d_out, ST * e + s + 1 + 2)
                    settle(pool)
                    pool.indirect_dma_start(
                        out=dst, out_offset=bass.IndirectOffsetOnAxis(ap=id_cur[:, s:s + 1], axis=0),
                        in_=stage[:, s, :], in_offset=None, bounds_check=N - 1, compute_op=add).then_inc(S.added, 16)
                pool.wait_ge(S.added, 16 * ST * e + 16 * ST)
                pool.sem_inc(S.landed, 1)

            def ffn(S, dst):
                weight_max(S, 0)
                with pool.Fori(0, STEPS) as i:
                    for b in range(2):
                        pool.wait_ge(S.stat_ready, 2 * i + b + 1)
                        pool.tensor_tensor(rstd[:, b, :], rstd[:, b, :], mhalf[:, :],
                                           ALU.pow).then_inc(S.rstd_ready, 1)
                pool.wait_ge(S.stored, 32 + 32 * STEPS)
                gather(S, 0)
                pool.wait_ge(S.kept, 16 * (STEPS if S is sems[0] else B * QUADS))
                pool.sem_inc(S.landed, 1)
                with pool.Fori(0, E - 1) as e:
                    expert(S, e, dst, False)
                expert(S, E - 1, dst, True)

            def attention():
                def norm_quad(b, j):
                    q = QUADS * b + j
                    pool.wait_ge(at.stat, q + 1)
                    pool.tensor_tensor(rstd[:, j % 2, :], rstd[:, j % 2, :], mhalf[:, :], ALU.pow).then_inc(at.rstd, 1)
                    pool.wait_ge(at.xn, q + 1)
                    settle(pool)
                    x_q = tiles(xs, G4 * q, G4)
                    pool.tensor_tensor(x_q, x_q, bc(bo_b[:, :], 1, G4), add).then_inc(at.bo, 1)

                def step(b, first, last):
                    for j in range(QUADS):
                        if not last:
                            nb, nj = next_quad(b, j)
                            if not (isinstance(nb, int) and nb == B):
                                norm_quad(nb, nj)
                        if j == 0 and not first:
                            pool.wait_ge(at.m_amax, b)
                            settle(pool)
                            pool.partition_all_reduce(mx2[:, 1:2], mx2[:, 0:1], P, RMAX).then_inc(at.m_max, 1)

                norm_quad(0, 0)
                batches(pool, step)

            ffn(sems[0], x1_d)
            attention()
            ffn(sems[1], of)

        @block.sync
        def _(sp):
            sp.dma_start(rw8[:, :], router_w).then_inc(s_rwld, 16)
            sp.dma_start(wq32[:, :, :], wq.rearrange("(k p) d -> p k d", p=P)).then_inc(s_rwld, 16)

            def pair(ap, i):
                return col(ap, i * PAIR, PAIR)

            def store_rows(S, i):
                for b in range(2):
                    sp.wait_ge(S.lo_ready, 2 * i + b + 1)
                    sp.dma_start(col(rows_v, i * PAIR + b * G4, G4), rows[:, b, :, :]).then_inc(S.stored, 16)

            def load_x(loaded, src_v, i):
                sp.dma_start(pair(xs, i), pair(src_v, i)).then_inc(loaded, 16)

            def ffn_in(S, src_v, keep_v):
                def keep(i):
                    sp.dma_start(pair(keep_v, i), pair(xs, i)).then_inc(S.kept, 16)
                    store_rows(S, i)

                load_x(S.loaded, src_v, 0)
                with sp.Fori(0, STEPS - 1) as i:
                    sp.wait_ge(S.loaded, 16 * i + 16)
                    load_x(S.loaded, src_v, i + 1)
                    keep(i)
                sp.wait_ge(S.loaded, 16 * STEPS)
                keep(STEPS - 1)

            def load_raw(S, n):
                src = raw_src(n)
                for m, (loaded, split) in enumerate(((S.raw_g, S.gu_lo), (S.raw_u, S.gu_lo), (S.raw_d, S.d_lo))):
                    sp.wait_ge(split, n * (4 if m < 2 else 2))
                    sp.dma_start(raw_dst[m], src[m]).then_inc(loaded, 16)

            def experts(S):
                with sp.Fori(0, E - 1) as e:
                    load_raw(S, e + 1)
                sp.wait_ge(S.landed, E + 1)

            ffn_in(sems[0], x_v, x1_v)
            for dst, src in ((wv32[:, :, :], wv.rearrange("(k p) d -> p k d", p=P)),
                             (wo32[:, :, :], wo.rearrange("(k p) d -> p k d", p=P)),
                             (bq_b[:, :], bq.unsqueeze(0).to_broadcast([P, D])),
                             (bo_b[:, :], bo.unsqueeze(0).to_broadcast([P, D]))):
                sp.dma_start(dst, src).then_inc(s_atw, 16)
            sp.dma_start(bv_p[:, :], bv.rearrange("(k p) -> p k", p=P), allow_slow_non_contiguous=True).then_inc(s_atw, 16)
            experts(sems[0])
            load_x(at.x1_in, x1_v, 0)
            with sp.Fori(0, STEPS - 1) as i:
                sp.wait_ge(at.x1_in, 16 * i + 16)
                load_x(at.x1_in, x1_v, i + 1)
            with sp.Fori(0, B * QUADS) as q:
                sp.wait_ge(at.x2, 2 * q + 2)
                sp.dma_start(col(o_v, q * G4, G4), col(xs, q * G4, G4)).then_inc(sems[1].kept, 16)
            with sp.Fori(0, STEPS) as i:
                store_rows(sems[1], i)
            experts(sems[1])

        @block.scalar
        def _(act):
            def split_hi(m, h, done):
                r, hi, _ = halves(m, h)
                act.activation(hi, r, ACT.Copy, scale=sc_next[:, m:m + 1] if m < 2 else sc_cur[:, 2:3]).then_inc(done, 1)

            def ffn_in(S):
                with act.Fori(0, STEPS) as i:
                    act.wait_ge(S.stored, 32 * i + 32)
                    for b in range(2):
                        act.wait_ge(S.xn_ready, 2 * i + b + 1)
                        act.activation(rows[:, b, :, 0:D], xn[:, b, :, :], ACT.Copy).then_inc(S.hi_ready, 1)
                    for k in range(4):
                        act.wait_ge(S.turned, 4 * i + k + 1)
                        if k >= 2:
                            act.wait_ge(S.logit_ready, 4 * i + k - 1)
                        act.activation(xt2_flat[:, k % 2, :], bank16[k % 2], ACT.Copy).then_inc(S.turned_ok, 1)
                    act.wait_ge(S.logit_ready, 4 * i + 4)
                    src = bank[2][:, 0:PAIR * E].rearrange("p (b g e) -> p g b e", b=2, g=G4)
                    act.activation(lg_gt[:, :, bass.ds(2 * i, 2), :], src, ACT.Copy,
                                   scale=rws[:, 6:7]).then_inc(S.logit_out, 1)

            def unit_silu(S, e, u):
                act.wait_ge(S.g_ready, UNITS * e + u + 1)
                act.wait_ge(S.h32_ready, UNITS * e + u + 1)
                act.activation(act_s[:, u % 2, :], bank[u % 2][:, 0:CW], ACT.Silu,
                               scale=sc_cur[:, 3:4]).then_inc(S.s_ready, 1)

            def unit_hi(S, e, u):
                f, c = divmod(u, CH)
                act.wait_ge(S.h32_ready, UNITS * e + u + 1 + 2)
                act.activation(hid[:, 0, f, c * CW:(c + 1) * CW], h32[:, u % HB, :], ACT.Copy).then_inc(S.hhi_ready, 1)

            def expert(S, e, last):
                act.wait_ge(S.cur_ready, e + 1)
                for u in range(UNITS):
                    unit_silu(S, e, u)
                    if u:
                        unit_hi(S, e, u - 1)
                    if u in (1, 3):
                        if u == 1:
                            act.wait_ge(S.raw_d, 16 * e + 16)
                            act.wait_ge(S.d_ready, ST * e + 1)
                        split_hi(2, u // 2, S.d_hi)
                    if not last and u in (24, 26):
                        if u == 24:
                            act.wait_ge(S.scales_ready, e + 2)
                        split_hi((u - 24) // 2, 0, S.gu_hi)
                unit_hi(S, e, UNITS - 1)
                for s in range(ST):
                    act.wait_ge(S.d_ready, ST * e + s + 1 + 1)
                    if s == 0:
                        act.wait_ge(S.landed, e + 1)
                        act.wait_ge(S.wfac_ready, e + 1)
                    act.activation(stage[:, s, :], bank[4 + s % 2][:, 0:D], ACT.Copy,
                                   scale=w_fac[:, s:s + 1]).then_inc(S.d_out, 1)
                    if not last and s in (1, 2):
                        split_hi(s - 1, 1, S.gu_hi)

            def ffn(S):
                src = raw_src(0)
                if S is sems[1]:
                    act.wait_ge(at.out, 2 * B * QUADS)
                for m, s in enumerate((S.raw_g, S.raw_u, S.raw_d)):
                    act.dma_start(raw_dst[m], src[m]).then_inc(s, 16)
                if S is sems[0]:
                    act.wait_ge(s_boot, 5)
                    act.activation(rwh[:, 0, :], rw8[:, :], ACT.Copy, scale=rws[0:E, 0:1]).then_inc(s_boota, 1)
                    act.activation(wq16[:, 0, :, :], wq32[:, :, :], ACT.Copy, scale=rws[:, 1:2]).then_inc(s_boota, 1)
                act.wait_ge(S.scales_ready, 1)
                for h in range(2):
                    for m in range(2):
                        split_hi(m, h, S.gu_hi)
                ffn_in(S)
                act.wait_ge(S.cent_ready, 1)
                act.activation(t1[:, :, :], lg[:, :, :], ACT.Exp).then_inc(S.ex_ready, 1)
                with act.Fori(0, E - 1) as e:
                    expert(S, e, False)
                expert(S, E - 1, True)

            def attention():
                def norm_hi(b, j):
                    q = QUADS * b + j
                    act.wait_ge(at.xn, q + 1)
                    wait_for(act, at.gt, q - 1)
                    act.activation(rows[:, j % 2, :, 0:D], xn[:, j % 2, :, :], ACT.Copy).then_inc(at.hi, 1)

                def xt_copy(b, j, k):
                    act.wait_ge(at.xt_turned, 2 * (QUADS * b + j) + k + 1)
                    act.activation(xt2_flat[:, k, :], bank16[0], ACT.Copy).then_inc(at.xt, 1)

                def qt_copy(b, j, k):
                    act.wait_ge(at.qt_turned, 2 * (QUADS * b + j) + k + 1)
                    t = G4 * j + 2 * k
                    act.activation(qT[:, t:t + 2].rearrange("p t c n -> p (t c n)"), bank16[1],
                                   ACT.Copy).then_inc(at.qt, 1)

                def step(b, first, last):
                    for j in range(QUADS):
                        q, r = QUADS * b + j, j % 2
                        nb, nj = next_quad(b, j)
                        more = not last and not (isinstance(nb, int) and nb == B)
                        if not last:
                            act.wait_ge(at.cent, q + 1)
                            act.activation(qb[:, r], qb[:, r], ACT.Exp).then_inc(at.ex, 1)
                        if more:
                            norm_hi(nb, nj)
                        if j == 0 and not first:
                            act.wait_ge(at.gt, q)
                            act.activation(gt_s, bank[4][:, :].rearrange("p (k d) -> p k d", k=KD), ACT.Copy,
                                           scale=1.0 / XSCALE).then_inc(at.gt_out, 1)
                        if more:
                            xt_copy(nb, nj, 0)
                        if not last:
                            act.wait_ge(at.qs, q + 1)
                            wait_for(act, at.qt_turned, 2 * (q - 1))
                            act.activation(qrow[:, r, :, 0:D], qb[:, r], ACT.Copy).then_inc(at.qhi, 1)
                            wait_for(act, at.eklo, q - 1)
                            act.activation(ekb[:, r], qb[:, r], ACT.Exp, scale=1.0 / QTOP)
                            wait_for(act, at.gt, q - 1)
                            act.activation(ekrow[:, r, :, 0:D], qb[:, r], ACT.Exp, scale=1.0 / QTOP).then_inc(at.ekhi, 1)
                        if more:
                            xt_copy(nb, nj, 1)
                        if j and not last or j == 0 and not first:
                            for k in range(2):
                                qt_copy(*((b, j - 1) if j else (b - 1, QUADS - 1)), k)
                        if j == 0 and not first:
                            act.wait_ge(at.m_scale, b)
                            act.activation(m2h[:, 0], m2f, ACT.Copy, scale=mx2[:, 2:3]).then_inc(at.m_hi, 1)

                norm_hi(0, 0)
                for k in range(2):
                    xt_copy(0, 0, k)
                batches(act, step)

            ffn(sems[0])
            attention()
            ffn(sems[1])

        @block.vector
        def _(dve):
            bs = Chain(dve, s_boot)
            dve.wait_ge(s_gstep, 4)
            bs.step(dve.tensor_reduce(sel8[:, :], ident[:, :].rearrange("p (t e) -> p e t", e=E), AX.X, add))
            bs.step(dve.tensor_copy(same_e[:, :].rearrange("p (t e) -> p t e", e=E), bc(sel8[:, :], 1, TC)))
            bs.step(dve.memset(rwa[:, :], 0.0))
            dve.wait_ge(s_rwld, 16 * 2)
            dve.tensor_reduce(rwa[:, 1:2], wq32[:, :, :].rearrange("p k d -> p (k d)"), AX.X, ALU.max,
                              apply_absolute_value=True)
            bs.step(dve.tensor_reduce(rwa[0:E, 0:1], rw8[:, :], AX.X, ALU.max, apply_absolute_value=True))
            dve.wait_ge(s_bootp, 1)
            bx = Chain(dve, s_bootx)
            scales(bx, dve, rws[:, 4:6], rws[:, 0:2], rws[:, 2:4])
            bs.step(dve.tensor_scalar(rws[:, 6:8], rws[:, 2:4], 1.0 / XSCALE, None, mult))
            dve.wait_ge(s_boota, 2)
            bs.step(dve.scalar_tensor_tensor(rwh[:, 1, :], rw8[:, :], rws[0:E, 0:1], rwh[:, 0, :], mult, sub))
            dve.wait_ge(s_bootpe, 1)
            bs.step(dve.tensor_copy(rwT[:, :, :, :].rearrange("p a k e -> p (a k e)"), bank16[7][:, 0:2 * KD * E]))
            bs.mark(dve.scalar_tensor_tensor(wq16[:, 1, :, :], wq32[:, :, :], rws[:, 1:2], wq16[:, 0, :, :], mult, sub))
            bs.mark(dve.memset(ones[:, :], 1.0))
            bs.step(dve.tensor_reduce(sel_h[:, :], ident[:, :].rearrange("p (h d) -> p h d", d=DH), AX.X, add))
            bs.step(dve.tensor_copy(same_h[:, :].rearrange("p (h d) -> p h d", d=DH), bc(sel_h[:, :], 2, DH)))

            def weight_amax(S, m, n):
                dve.wait_ge((S.raw_g, S.raw_u, S.raw_d)[m], 16 * n + 16)
                dve.tensor_reduce(am[:, m:m + 1], raw[m], AX.X, ALU.max,
                                  apply_absolute_value=True).then_inc(S.amax_ready, 1)

            def weight_scales(S, ch, n):
                dve.wait_ge(S.amax_all, n + 1)
                scales(ch, dve, amr[:, :], sc_next[:, 0:3], sc_next[:, 3:6])
                dve.tensor_copy(spare_v[:, :], sc_next[:, 0:1]).then_inc(S.scales_ready, 1)

            def split_lo(m, h, done):
                r, hi, lo = halves(m, h)
                dve.scalar_tensor_tensor(lo, r, sc_next[:, m:m + 1] if m < 2 else sc_cur[:, 2:3], hi,
                                         mult, sub).then_inc(done, 1)

            def ffn_in(S, ch, wait_x):
                ch_per = 16
                with dve.Fori(0, STEPS) as i:
                    ch.enter(i, ch_per)
                    wait_x(i)
                    for b in range(2):
                        for g in range(G4):
                            v = ch.mark(dve.bn_stats(bst[:, b, g, :], xs[:, bass.ds(i * PAIR + b * G4 + g, 1), :]))
                    ch.wait()
                    settle(dve)
                    for b in range(2):
                        for g in range(G4):
                            ch.mark(dve.bn_aggr(mv[:, b, g, :], bst[:, b, g, :]))
                    ch.wait()
                    for b in range(2):
                        dve.tensor_scalar(rstd[:, b, :], mv[:, b, :, 1], EPS, XSCALE ** -2, add,
                                          mult).then_inc(S.stat_ready, 1)
                    for b in range(2):
                        dve.wait_ge(S.rstd_ready, 2 * i + b + 1)
                        for g in range(G4):
                            last = dve.tensor_scalar(xn[:, b, g, :], xs[:, bass.ds(i * PAIR + b * G4 + g, 1), :],
                                                     mv[:, b, g, 0:1], rstd[:, b, g:g + 1], sub, mult)
                        last.then_inc(S.xn_ready, 1)
                    for b in range(2):
                        dve.wait_ge(S.hi_ready, 2 * i + b + 1)
                        dve.wait_ge(S.xn_ready, 2 * i + b + 1)
                        dve.tensor_tensor(rows[:, b, :, D:2 * D], xn[:, b, :, :], rows[:, b, :, 0:D],
                                          sub).then_inc(S.lo_ready, 1)
                    ch.leave(STEPS)

            def route(S, ch):
                dve.wait_ge(S.logit_out, STEPS + 1)
                ch.step(dve.tensor_reduce(v1[:, :], lg[:, :, :], AX.X, ALU.max))
                dve.tensor_tensor(lg[:, :, :], lg[:, :, :], bc(v1[:, :], 2, E), sub).then_inc(S.cent_ready, 1)
                dve.wait_ge(S.ex_ready, 1)
                ch.step(dve.tensor_reduce(v1[:, :], t1[:, :, :], AX.X, add))
                ch.step(dve.reciprocal(v1[:, :], v1[:, :]))
                ch.step(dve.tensor_tensor(t1[:, :, :], t1[:, :, :], bc(v1[:, :], 2, E), mult))
                prob, mask, rest = t1, t2, t3

                def pick(p, top, dst):
                    ch.step(dve.tensor_reduce(top, p, AX.X, ALU.max))
                    ch.step(dve.tensor_tensor(dst, p, bc(top, 2, E), ALU.is_equal))
                    ch.step(dve.tensor_tensor(dst, dst, bc(edesc[:, :], 1, NT), mult))
                    ch.step(dve.tensor_reduce(v2[:, :], dst, AX.X, ALU.max))
                    ch.step(dve.tensor_tensor(dst, dst, bc(v2[:, :], 2, E), ALU.is_equal))

                pick(prob[:, :, :], v1[:, :], mask[:, :, :])
                ch.step(dve.scalar_tensor_tensor(rest[:, :, :], mask[:, :, :], -2.0, prob[:, :, :], mult, add))
                pick(rest[:, :, :], v3[:, :], lg[:, :, :])
                ch.step(dve.tensor_tensor(mask[:, :, :], mask[:, :, :], lg[:, :, :], add))
                ch.step(dve.tensor_tensor(v1[:, :], v1[:, :], v3[:, :], add))
                ch.step(dve.tensor_scalar(v1[:, :], v1[:, :], 1e-6, None, add))
                ch.step(dve.reciprocal(v1[:, :], v1[:, :]))
                ch.step(dve.tensor_tensor(prob[:, :, :], prob[:, :, :], mask[:, :, :], mult))
                dve.tensor_tensor(prob[:, :, :], prob[:, :, :], bc(v1[:, :], 2, E), mult).then_inc(S.w_ready, 1)
                dve.wait_ge(S.w_ready, 1)
                parts = [val[:, :, :, 2 + k].rearrange("p e t -> p t e") for k in range(3)]
                ch.step(dve.tensor_copy(parts[0], prob[:, :, :]))
                ch.step(dve.tensor_tensor(rest[:, :, :], prob[:, :, :], parts[0], sub))
                ch.step(dve.tensor_copy(parts[1], rest[:, :, :]))
                ch.mark(dve.tensor_tensor(parts[2], rest[:, :, :], parts[1], sub))
                dve.wait_ge(S.wt_turned, 1)
                ch.mark(dve.tensor_copy(wT[:, :], bank[3][:, :]))
                ch.step(dve.memset(cand[:, :], 1 << 29))
                with dve.Fori(0, 30) as r:
                    ch.enter(r, 2)
                    dve.tensor_scalar(kT[:, :], wT[:, :], cand[:, :].bitcast(f32), None, ALU.is_ge, add,
                                      accum_out=cnt[:, 0:1]).then_inc(S.compared, 1)
                    dve.wait_ge(S.counted, r + 1)
                    ch.step(dve.tensor_scalar(flip[:, :], bank[4][:, 0:1], float(C), bit_f[:, bass.ds(r + 1, 1)],
                                              ALU.is_lt, mult))
                    ch.step(dve.scalar_tensor_tensor(cand[:, :], flip[:, :], bit_i[:, bass.ds(r + 2, 1)], cand[:, :],
                                                     ALU.bitwise_xor, ALU.bitwise_xor))
                    ch.leave(30)
                thr = cand[:, :].bitcast(f32)
                ch.mark(dve.tensor_scalar(kT[:, :], wT[:, :], thr, None, ALU.is_gt, add, accum_out=cnt[:, 0:1]))
                dve.tensor_scalar(rT[:, :], wT[:, :], thr, None, ALU.is_equal, add,
                                  accum_out=cnt[:, 1:2]).then_inc(S.ranked, 1)
                dve.wait_ge(S.offset_ready, 1)
                ch.mark(dve.tensor_scalar(tot[:, 0:1], bank[4][:, 0:1], -1.0, float(C), mult, add))
                ch.step(dve.tensor_copy(tot[:, 1:2], bank[4][:, 1:2]))
                ch.step(dve.tensor_tensor_scan(wT[:, :], rT[:, :], rT[:, :], tot[:, 1:2], add, ALU.max))
                ch.step(dve.scalar_tensor_tensor(rT[:, :], wT[:, :], tot[:, 0:1], rT[:, :], ALU.is_le, mult))
                ch.step(dve.tensor_tensor(kT[:, :], kT[:, :], rT[:, :], add))
                dve.tensor_tensor_scan(wT[:, :], kT[:, :], kT[:, :], 0.0, add, ALU.max).then_inc(S.ranked, 1)
                dve.wait_ge(S.offset_ready, 2)
                ch.step(dve.tensor_copy(tot[:, 2:3], bank[4][:, 2:3]))
                dve.scalar_tensor_tensor(rT[:, :], wT[:, :], tot[:, 2:3], kT[:, :], add, mult).then_inc(S.slots_ready, 1)
                dve.wait_ge(S.back_turned, 1)
                vi, ai = t2[:, :, :].bitcast(i32), t3[:, :, :].bitcast(i32)
                ch.step(dve.tensor_scalar(vi.rearrange("p t e -> p (t e)"), bank[5][:, :], float(P - 1), None, add))
                ch.step(dve.tensor_scalar(ai, vi, P - 1, None, ALU.bitwise_and))
                ch.mark(dve.tensor_copy(pos_a[:, :, :].rearrange("p e t -> p t e"), ai))
                ch.step(dve.tensor_scalar(vi, vi, 7, None, ALU.logical_shift_right))
                ch.step(dve.tensor_copy(pos_b[:, :, :].rearrange("p e t -> p t e"), vi))

            def list_piece(S, ch, n, i):
                r, at = i % 2, slice(i * LT, (i + 1) * LT)
                pa, pb, vv = (col(a, n)[:, 0] for a in (pos_a[:, :, at], pos_b[:, :, at], val[:, :, at, :]))
                dve.wait_ge(S.piece_used, LP * n + i + 1)
                dve.tensor_tensor(hot_a[:, r], bc(pa, 1, P), slot_a[:, :, :], ALU.is_equal)
                ch.step(dve.tensor_tensor(hot_b[:, r], bc(slot_b[:, :], 1, LT), bc(pb, 2, ST), ALU.is_equal))
                dve.tensor_tensor(hot_v[:, r], bc(hot_b[:, r], 2, 5), bc(vv, 3, ST), mult).then_inc(S.piece_ready, 1)

            def list_read(S, ch, n):
                dve.wait_ge(S.piece_used, LP * n + LP + 2)
                ch.step(dve.tensor_copy(lst[:, :], bank[6][:, 0:5 * ST]))
                ch.mark(dve.tensor_tensor(w_tmp[:, :], lst[:, 2 * ST:3 * ST], lst[:, 3 * ST:4 * ST], add))
                ch.wait()
                ch.mark(dve.tensor_tensor(w_next[:, :], w_tmp[:, :], lst[:, 4 * ST:5 * ST], add))
                dve.scalar_tensor_tensor(id_next[:, :], lst[:, 0:ST], float(P), lst[:, ST:2 * ST], mult,
                                         add).then_inc(S.ids_ready, 1)

            def xt_read(S, n, j):
                dve.wait_ge(S.xt_turned, ST // 2 * n + j + 1)
                dst = xT[:, :, 2 * j * P:(2 * j + 2) * P].rearrange("p c (t n) -> p t c n", t=2)
                src = bank16[7].rearrange("p (t c n) -> p t c n", t=2, c=2 * KD)
                dve.tensor_copy(dst, src).then_inc(S.xt_ready, 1)

            def unit(S, e, u):
                dve.wait_ge(S.u_ready, UNITS * e + u + 1)
                dve.wait_ge(S.s_ready, UNITS * e + u + 1 + 2)
                dve.wait_ge(S.h_ready, UNITS * e + u + 1)
                dve.scalar_tensor_tensor(h32[:, u % HB, :], bank[2 + u % 2][:, 0:CW], sc_cur[:, 4:5], act_s[:, u % 2, :],
                                         mult, mult).then_inc(S.h32_ready, 1)

            def unit_lo(S, e, u):
                f, c = divmod(u, CH)
                dve.wait_ge(S.hhi_ready, UNITS * e + u + 1)
                dve.tensor_tensor(hid[:, 1, f, c * CW:(c + 1) * CW], h32[:, u % HB, :],
                                  hid[:, 0, f, c * CW:(c + 1) * CW], sub).then_inc(S.h_ready, 1)

            def expert(S, ch, e, last):
                n = e + 1
                ch.mark(dve.tensor_copy(sc_cur[:, 2:3], sc_next[:, 2:3]))
                ch.mark(dve.tensor_scalar(sc_cur[:, 4:5], sc_next[:, 0:1], HSHIFT, None, mult))
                ch.mark(dve.tensor_scalar(sc_cur[:, 5:6], sc_next[:, 3:4], sc_next[:, 4:5], sc_next[:, 5:6], mult, mult))
                ch.wait()
                dve.tensor_scalar(sc_cur[:, 3:4], sc_next[:, 3:4], 1.0 / XSCALE, None, mult).then_inc(S.cur_ready, 1)
                for u in range(UNITS):
                    unit(S, e, u)
                    if u:
                        unit_lo(S, e, u - 1)
                    if u in (2, 4):
                        dve.wait_ge(S.d_hi, 2 * e + u // 2)
                        split_lo(2, u // 2 - 1, S.d_lo)
                    if u == 5:
                        dve.wait_ge(S.landed, e + 1)
                        ch.mark(dve.tensor_copy(id_cur[:, :], id_next[:, :]))
                        dve.tensor_scalar(w_fac[:, :], w_next[:, :], sc_cur[:, 5:6], 0.5 / (HSHIFT * XSCALE), mult,
                                          mult).then_inc(S.wfac_ready, 1)
                    if last:
                        continue
                    if u in (7, 11, 15):
                        weight_amax(S, (u - 7) // 4, n)
                    if u in PIECE_AT:
                        list_piece(S, ch, n, PIECE_AT[u])
                    if u == 21:
                        weight_scales(S, ch, n)
                    if u == 24:
                        list_read(S, ch, n)
                    if u in (25, 27):
                        dve.wait_ge(S.gu_hi, 4 * n + (u - 23) // 2)
                        split_lo((u - 25) // 2, 0, S.gu_lo)
                unit_lo(S, e, UNITS - 1)
                if not last:
                    for m in range(2):
                        dve.wait_ge(S.gu_hi, 4 * n + 3 + m)
                        split_lo(m, 1, S.gu_lo)
                    for j in range(ST // 2):
                        xt_read(S, n, j)

            def ffn(S, wait_x):
                ch = Chain(dve, S.dstep)
                for m in range(3):
                    weight_amax(S, m, 0)
                weight_scales(S, ch, 0)
                for k in range(4):
                    dve.wait_ge(S.gu_hi, k + 1)
                    split_lo(k % 2, k // 2, S.gu_lo)
                ffn_in(S, ch, wait_x)
                route(S, ch)
                for i in range(LP):
                    list_piece(S, ch, 0, i)
                list_read(S, ch, 0)
                for j in range(ST // 2):
                    xt_read(S, 0, j)
                with dve.Fori(0, E - 1) as e:
                    ch.enter(e, EXPERT_STEPS)
                    expert(S, ch, e, False)
                    ch.leave(E - 1)
                expert(S, ch, E - 1, True)

            def attention():
                ch = Chain(dve, at.dstep)
                dve.wait_ge(s_atw, 16 * 5)
                for k in range(KD):
                    ch.mark(dve.tensor_scalar(mbv[:, k, :], same_h[:, :], bv_p[:, k:k + 1], None, mult))
                dve.wait_ge(at.a, 1)
                ch.step(dve.tensor_scalar(bvo[:, :, :].rearrange("p k d -> p (k d)"), bank[7][:, :], HS, None, mult))

                def norm(b, j):
                    q, r = QUADS * b + j, j % 2
                    dve.wait_ge(at.x1_in, 16 * (2 * b + j // 2 + 1))
                    wait_for(dve, at.lo, q - 1)
                    for g in range(G4):
                        ch.mark(dve.bn_stats(bst[:, r, g, :], tiles(xs, G4 * q + g, 1)[:, 0]))
                    ch.wait()
                    settle(dve)
                    for g in range(G4):
                        ch.mark(dve.bn_aggr(mv[:, r, g, :], bst[:, r, g, :]))
                    ch.wait()
                    dve.tensor_scalar(rstd[:, r, :], mv[:, r, :, 1], EPS, XSCALE ** -2, add, mult).then_inc(at.stat, 1)

                def norm_x(b, j):
                    q, r = QUADS * b + j, j % 2
                    dve.wait_ge(at.rstd, q + 1)
                    for g in range(G4):
                        last = dve.tensor_scalar(xn[:, r, g, :], tiles(xs, G4 * q + g, 1)[:, 0], mv[:, r, g, 0:1],
                                                 rstd[:, r, g:g + 1], sub, mult)
                    last.then_inc(at.xn, 1)

                def norm_lo(b, j):
                    q, r = QUADS * b + j, j % 2
                    dve.wait_ge(at.xn, q + 1)
                    dve.wait_ge(at.hi, q + 1)
                    dve.tensor_tensor(rows[:, r, :, D:2 * D], xn[:, r, :, :], rows[:, r, :, 0:D], sub).then_inc(at.lo, 1)

                def finish(b, j):
                    q = QUADS * b + j
                    for k in range(2):
                        if k == 0:
                            dve.wait_ge(at.bo, q + 1)
                        dve.wait_ge(at.out, 2 * q + k + 1)
                        settle(dve)
                        x_k = tiles(xs, G4 * q + 2 * k, 2)
                        dve.scalar_tensor_tensor(x_k, bank[6 + k][:, :].rearrange("p (t d) -> p t d", t=2), mx2[:, 4:5],
                                                 x_k, mult, add).then_inc(at.x2, 1)

                def step(b, first, last):
                    for j in range(QUADS):
                        q, r = QUADS * b + j, j % 2
                        nb, nj = next_quad(b, j)
                        more = not last and not (isinstance(nb, int) and nb == B)
                        q3 = qb[:, r].rearrange("p t (h d) -> p (t h) d", d=DH)
                        if not last:
                            wait_for(dve, at.eklo, q - 1)
                            for k in range(2):
                                dve.wait_ge(at.q, 2 * q + k + 1)
                                i = dve.scalar_tensor_tensor(qb[:, r, 2 * k:2 * k + 2],
                                                             bank[2 + k][:, :].rearrange("p (t d) -> p t d", t=2),
                                                             rws[:, 7:8], bc(bq_b[:, :], 1, 2), mult, add)
                            i.then_inc(at.qout, 1)
                            dve.wait_ge(at.qout, q + 1)
                            ch.step(dve.tensor_reduce(qmax[:, :], q3, AX.X, ALU.max))
                            dve.tensor_tensor(q3, q3, bc(qmax[:, :], 2, DH), sub).then_inc(at.cent, 1)
                        if more:
                            norm(nb, nj)
                        if j == 0 and not first:
                            dve.wait_ge(at.gt, q)
                            ch.step(dve.reciprocal(zr[:, :], bank[5][:, 0:KD]))
                            ch.mark(dve.tensor_scalar(zr[:, :], zr[:, :], HS, None, mult))
                        if more:
                            norm_x(nb, nj)
                        if not last:
                            dve.wait_ge(at.ex, q + 1)
                            ch.step(dve.tensor_reduce(qmax[:, :], q3, AX.X, add))
                            ch.step(dve.reciprocal(qmax[:, :], qmax[:, :]))
                            dve.scalar_tensor_tensor(q3, q3, HS * QTOP, bc(qmax[:, :], 2, DH), mult,
                                                     mult).then_inc(at.qs, 1)
                        if more:
                            norm_lo(nb, nj)
                        if j == 0 and not first:
                            dve.wait_ge(at.ctx, b)
                            dve.tensor_tensor(ctm, bank[6][:, 0:KD * P].rearrange("p (k d) -> p k d", k=KD),
                                              bc(same_h[:, :], 1, KD), mult).then_inc(at.ctm, 1)
                        for f in FINISH[j]:
                            if not first:
                                finish(b - 1, f)
                        if not last:
                            dve.wait_ge(at.qs, q + 1)
                            dve.wait_ge(at.qhi, q + 1)
                            dve.tensor_tensor(qrow[:, r, :, D:2 * D], qb[:, r], qrow[:, r, :, 0:D], sub).then_inc(at.qlo, 1)
                            dve.wait_ge(at.ekhi, q + 1)
                            dve.tensor_tensor(ekrow[:, r, :, D:2 * D], ekb[:, r], ekrow[:, r, :, 0:D],
                                              sub).then_inc(at.eklo, 1)
                        if j == 0 and not first:
                            dve.wait_ge(at.a, b + 1)
                            for k in range(KD):
                                ch.mark(dve.scalar_tensor_tensor(m2f[:, k, :], bank[7][:, k * D:(k + 1) * D], zr[:, k:k + 1],
                                                                 bvo[:, k, :], mult, add))
                            ch.wait()
                            dve.tensor_reduce(mx2[:, 0:1], m2f, AX.XY, ALU.max,
                                              apply_absolute_value=True).then_inc(at.m_amax, 1)
                            dve.wait_ge(at.m_max, b)
                            scales(ch, dve, mx2[:, 1:2], mx2[:, 2:3], mx2[:, 3:4])
                            dve.tensor_scalar(mx2[:, 4:5], mx2[:, 3:4], 1.0 / QTOP, None, mult).then_inc(at.m_scale, 1)
                            dve.wait_ge(at.m_hi, b)
                            dve.scalar_tensor_tensor(m2h[:, 1], m2f, mx2[:, 2:3], m2h[:, 0], mult, sub).then_inc(at.m_lo, 1)

                def looped(b, first, last):
                    if isinstance(b, int):
                        step(b, first, last)
                    else:
                        ch.enter(b - 1, LOOP_STEPS)
                        step(b, first, last)
                        ch.leave(B - 2)

                norm(0, 0)
                norm_x(0, 0)
                norm_lo(0, 0)
                batches(dve, looped)

            ffn(sems[0], lambda i: dve.wait_ge(sems[0].loaded, 16 * i + 16))
            attention()
            ffn(sems[1], lambda i: dve.wait_ge(at.x2, 4 * i + 4))

        @block.tensor
        def _(pe):
            pe.wait_ge(s_gstep, 4)
            pe.wait_ge(s_boot, 6)
            for a in range(2):
                for k in range(KD):
                    o = (a * KD + k) * E
                    last = pe.transpose(bank16[7][:, o:o + E], rwh[:, a, k * P:(k + 1) * P], ident16[0:E, 0:E])
            last.then_inc(s_bootpe, 1)
            pe.wait_ge(s_boot, 7)
            HALVES = ((0, 0), (0, 1), (1, 0))

            def turn(S, i, k):
                b, t0 = k // 2, 2 * (k % 2)
                if k % 2 == 0:
                    pe.wait_ge(S.lo_ready, 2 * i + b + 1)
                pe.wait_ge(S.turned_ok, 4 * i + k + 1)
                for t in range(2):
                    for c in range(2 * KD):
                        o = (t * 2 * KD + c) * P
                        last = pe.transpose(bank16[k % 2][:, o:o + P], rows[:, b, t0 + t, c * P:(c + 1) * P],
                                            ident16[:, :])
                last.then_inc(S.turned, 1)

            def logits(S, i, k):
                if k == 0:
                    pe.wait_ge(S.logit_out, i + 1)
                pe.wait_ge(S.turned_ok, 4 * i + k + 1 + 2)
                for t in range(2):
                    o = (2 * k + t) * E
                    for j, (a, w) in enumerate(HALVES):
                        for d in range(KD):
                            last = pe.matmul(bank[2][:, o:o + E], xt2[:, k % 2, t, a * KD + d, :], rwT[:, w, d, :],
                                             start=(j == 0 and d == 0), stop=(j == 2 and d == KD - 1))
                last.then_inc(S.logit_ready, 1)

            def ffn_in(S):
                with pe.Fori(0, STEPS) as i:
                    turn(S, i, 0)
                    turn(S, i, 1)
                    logits(S, i, 0)
                    turn(S, i, 2)
                    logits(S, i, 1)
                    turn(S, i, 3)
                    logits(S, i, 2)
                    logits(S, i, 3)

            def route(S):
                pe.wait_ge(s_const, 1)
                pe.wait_ge(S.w_ready, 1)
                wflat = t1[:, :, :].rearrange("p t e -> p (t e)")
                for g in range(G4):
                    last = pe.transpose(bank[3][:, g * P:(g + 1) * P], wflat[:, g * P:(g + 1) * P], ident[:, :])
                last.then_inc(S.wt_turned, 1)
                with pe.Fori(0, 30) as r:
                    pe.wait_ge(S.compared, r + 1)
                    pe.matmul(bank[4][:, 0:1], same_e[:, :], cnt[:, 0:1], start=True, stop=True).then_inc(S.counted, 1)
                pe.wait_ge(S.ranked, 1)
                pe.matmul(bank[4][:, 0:1], same_e[:, :], cnt[:, 0:1], start=True, stop=True)
                pe.matmul(bank[4][:, 1:2], before_e[:, :], cnt[:, 1:2], start=True, stop=True).then_inc(S.offset_ready, 1)
                pe.wait_ge(S.ranked, 2)
                pe.matmul(bank[4][:, 2:3], before_e[:, :], wT[:, 4 * P - 1:4 * P], start=True,
                          stop=True).then_inc(S.offset_ready, 1)
                pe.wait_ge(S.slots_ready, 1)
                for g in range(G4):
                    last = pe.transpose(bank[5][:, g * P:(g + 1) * P], rT[:, g * P:(g + 1) * P], ident[:, :])
                last.then_inc(S.back_turned, 1)

            def list_piece(S, n, i):
                pe.wait_ge(S.piece_ready, LP * n + i + 1)
                for t in range(LT):
                    last = pe.matmul(bank[6][:, 0:5 * ST], hot_a[:, i % 2, :, t],
                                     hot_v[:, i % 2, t].rearrange("p v s -> p (v s)"),
                                     start=(i == 0 and t == 0), stop=(i == LP - 1 and t == LT - 1))
                last.then_inc(S.piece_used, 1)

            def xt_turn(S, n, j):
                pe.wait_ge(gathered[j], 32 * (n + S.first) + 32)
                pe.wait_ge(S.xt_ready, ST // 2 * n + j + 1)
                for t in range(2):
                    for c in range(2 * KD):
                        o = (t * 2 * KD + c) * P
                        last = pe.transpose(bank16[7][:, o:o + P], gat[:, 2 * j + t, c * P:(c + 1) * P], ident16[:, :])
                last.then_inc(S.xt_turned, 1)

            def expert(S, e, last):
                n = e + 1
                pe.wait_ge(S.xt_ready, ST // 2 * (e + 1) + 1)
                for u in range(UNITS):
                    f, c = divmod(u, CH)
                    if u in (0, UNITS // 2):
                        pe.wait_ge(S.gu_lo, 4 * e + (2 if u == 0 else 4))
                    for m, (free, done) in enumerate(((S.s_ready, S.g_ready), (S.h32_ready, S.u_ready))):
                        pe.wait_ge(free, UNITS * e + u + 1)
                        for j, (a, w) in enumerate(HALVES):
                            for k in range(KD):
                                mm = pe.matmul(bank[2 * m + u % 2][:, 0:CW], wgu[m][:, w, k, f * P:(f + 1) * P],
                                               xT[:, a * KD + k, c * CW:(c + 1) * CW],
                                               start=(j == 0 and k == 0), stop=(j == 2 and k == KD - 1))
                        mm.then_inc(done, 1)
                    if not last and u in PE_PIECE_AT:
                        list_piece(S, n, PE_PIECE_AT[u])
                pe.wait_ge(S.d_lo, 2 * e + 2)
                for s in range(ST):
                    chunk = ((s + 1) * P - 1) // CW
                    pe.wait_ge(S.h_ready, UNITS * e + UNITS - CH + chunk + 1 + HB)
                    pe.wait_ge(S.d_out, ST * e + s + 1)
                    for f in range(FT):
                        for j, (a, w) in enumerate(HALVES):
                            mm = pe.matmul(bank[4 + s % 2][:, 0:D], hid[:, a, f, s * P:(s + 1) * P], wdn[:, w, f, :],
                                           start=(f == 0 and j == 0), stop=(f == FT - 1 and j == 2))
                    mm.then_inc(S.d_ready, 1)
                    if not last and XT_AT <= s < XT_AT + ST // 2:
                        xt_turn(S, n, s - XT_AT)

            def ffn(S):
                ffn_in(S)
                route(S)
                for i in range(LP):
                    list_piece(S, 0, i)
                for j in range(ST // 2):
                    xt_turn(S, 0, j)
                with pe.Fori(0, E - 1) as e:
                    expert(S, e, False)
                expert(S, E - 1, True)

            def attention():
                for k in range(KD):
                    if k == 0:
                        pe.wait_ge(at.dstep, KD)
                    i = pe.matmul(bank[7][:, k * D:(k + 1) * D], mbv[:, k, :], wo32[:, k, :], start=True, stop=True)
                i.then_inc(at.a, 1)

                def turn_x(b, j, k):
                    q = QUADS * b + j
                    if k == 0:
                        pe.wait_ge(at.lo, q + 1)
                    wait_for(pe, at.xt, 2 * q + k)
                    for t in range(2):
                        for c in range(2 * KD):
                            o = (t * 2 * KD + c) * P
                            i = pe.transpose(bank16[0][:, o:o + P], rows[:, j % 2, 2 * k + t, c * P:(c + 1) * P],
                                             ident16[:, :])
                    i.then_inc(at.xt_turned, 1)

                def turn_q(b, j, k):
                    q = QUADS * b + j
                    if k == 0:
                        pe.wait_ge(at.qlo, q + 1)
                    wait_for(pe, at.qt, 2 * q + k)
                    for t in range(2):
                        for c in range(2 * KD):
                            o = (t * 2 * KD + c) * P
                            i = pe.transpose(bank16[1][:, o:o + P], qrow[:, j % 2, 2 * k + t, c * P:(c + 1) * P],
                                             ident16[:, :])
                    i.then_inc(at.qt_turned, 1)

                def queries(b, j):
                    q = QUADS * b + j
                    wait_for(pe, at.qout, q)
                    for k in range(2):
                        pe.wait_ge(at.xt, 2 * q + k + 1)
                        for t in range(2):
                            for n, (a, w) in enumerate(HALVES):
                                for d in range(KD):
                                    i = pe.matmul(bank[2 + k][:, t * D:(t + 1) * D], xt2[:, k, t, a * KD + d, :],
                                                  wq16[:, w, d, :], start=(n == 0 and d == 0), stop=(n == 2 and d == KD - 1))
                        i.then_inc(at.q, 1)

                def keys(b, j):
                    pe.wait_ge(at.eklo, QUADS * b + j + 1)
                    for t in range(G4):
                        for m in range(KD):
                            for n, (a, w) in enumerate(HALVES):
                                pe.matmul(bank[4][:, m * D:(m + 1) * D], rows[:, j % 2, t, a * D + m * P:a * D + (m + 1) * P],
                                          ekrow[:, j % 2, t, w * D:(w + 1) * D], start=(j == t == m == n == 0),
                                          stop=(j == QUADS - 1 and t == G4 - 1 and m == KD - 1 and n == 2))
                            for a in range(2):
                                i = pe.matmul(bank[5][:, m:m + 1], ekrow[:, j % 2, t, a * D + m * P:a * D + (m + 1) * P],
                                              ones[:, :], start=(j == t == m == a == 0),
                                              stop=(j == QUADS - 1 and t == G4 - 1 and m == KD - 1 and a == 1))
                    i.then_inc(at.gt, 1)

                def finish(b, j):
                    q = QUADS * b + j
                    if j == 0:
                        pe.wait_ge(at.m_lo, b + 1)
                    for k in range(2):
                        pe.wait_ge(at.qt, 2 * q + k + 1)
                        if j:
                            pe.wait_ge(at.x2, 2 * q + k - 1)
                        for t in range(2):
                            for n, (a, w) in enumerate(HALVES):
                                for d in range(KD):
                                    i = pe.matmul(bank[6 + k][:, t * D:(t + 1) * D], qT[:, G4 * j + 2 * k + t, a * KD + d, :],
                                                  m2h[:, w, d, :], start=(n == 0 and d == 0), stop=(n == 2 and d == KD - 1))
                        i.then_inc(at.out, 1)

                def step(b, first, last):
                    for j in range(QUADS):
                        nb, nj = next_quad(b, j)
                        more = not last and not (isinstance(nb, int) and nb == B)
                        before = (b, j - 1) if j else (b - 1, QUADS - 1)
                        one_back = j and not last or j == 0 and not first
                        if not last:
                            queries(b, j)
                        if one_back:
                            keys(*before)
                        for f in FINISH[j]:
                            if not first:
                                finish(b - 1, f)
                        for k in range(2):
                            if more:
                                turn_x(nb, nj, k)
                            if one_back:
                                turn_q(*before, k)
                        if j == 0 and not first:
                            pe.wait_ge(at.gt_out, b)
                            for m in range(KD):
                                for k in range(KD):
                                    i = pe.matmul(bank[6][:, m * P:(m + 1) * P], wv32[:, k, m * P:(m + 1) * P],
                                                  gt_s[:, k, m * P:(m + 1) * P], start=(k == 0), stop=(k == KD - 1))
                            i.then_inc(at.ctx, 1)
                            pe.wait_ge(at.ctm, b)
                            for k in range(KD):
                                i = pe.matmul(bank[7][:, k * D:(k + 1) * D], ctm[:, k, :], wo32[:, k, :], start=True, stop=True)
                            i.then_inc(at.a, 1)

                for k in range(2):
                    turn_x(0, 0, k)
                batches(pe, step)

            ffn(sems[0])
            attention()
            pe.wait_ge(at.qout, B * QUADS)
            ffn(sems[1])


_INS = ['L0_attn_x', 'L0_attn_Wq', 'L0_attn_bq', 'L0_attn_Wv', 'L0_attn_bv', 'L0_attn_Wo', 'L0_attn_bo',
        'L0_ffn_router_w', 'L0_ffn_wg', 'L0_ffn_wu', 'L0_ffn_wd']


def kernel(**inputs):
    import numpy as _np
    import concourse.bacc as _bacc
    from concourse import mybir as _mybir
    from concourse.bass_utils import run_bass_kernel_spmd as _run

    nc = _bacc.Bacc("TRN2", target_bir_lowering=False, num_devices=1)
    arrays, args = {}, []
    for name in _INS:
        a = _np.ascontiguousarray(inputs[name])
        arrays[f"in_{name}"] = a
        args.append(nc.dram_tensor(f"in_{name}", a.shape, _mybir.dt.from_np(a.dtype), kind="ExternalInput").ap())
    x = arrays["in_L0_attn_x"]
    out = nc.dram_tensor("out_x", x.shape, _mybir.dt.from_np(x.dtype), kind="ExternalOutput").ap()
    macaron_block(nc, *args, out)
    r = _run(nc, [arrays], core_ids=[0])
    return r.results[0]["out_x"]
```

```python
import concourse.bass as bass
from concourse import mybir
from contextlib import ExitStack
from collections import namedtuple


def macaron_block(nc, x, wq, bq, wv, bv, wo, bo, router_w, wg, wu, wd, out):
    f32, f16, b16, i32, u32 = (mybir.dt.float32, mybir.dt.float16, mybir.dt.bfloat16,
                               mybir.dt.int32, mybir.dt.uint32)
    ALU, ACT, AX = mybir.AluOpType, mybir.ActivationFunctionType, mybir.AxisListType
    add, sub, mult = ALU.add, ALU.subtract, ALU.mult

    P = 128
    B, SEQ, D = x.shape
    N = B * SEQ
    E, _, F = wg.shape
    C = int(1.25 * N / E)
    NT = N // P
    KD = D // P
    FT = F // P
    H = 16
    DH = D // H
    HS = float((DH ** 0.5) ** -0.25)
    QTOP = 2.0 ** 14
    BT = SEQ // P
    QUADS = BT // 4
    ST = C // P
    CH = 4
    CW = C // CH
    HB = 4
    UNITS = FT * CH
    G4 = 4
    PAIR = 2 * G4
    STEPS = NT // PAIR
    TC = NT // G4
    LT = 8
    LP = NT // LT
    EPS = 1e-5
    XSCALE = 2.0 ** 10
    WTOP = 13
    LOOP_STEPS = 56
    HSHIFT = 2.0 ** -39
    ROUNDS = 15
    ONE = 1 << 23

    xf = x.rearrange("b n d -> (b n) d")
    of = out.rearrange("b n d -> (b n) d")
    x_v = xf.rearrange("(t p) d -> p t d", p=P)
    o_v = of.rearrange("(t p) d -> p t d", p=P)

    ctx = ExitStack()
    with ctx:
        def sb(name, shape, dt):
            return ctx.enter_context(nc.sbuf_tensor(name, shape, dt))

        def sem(name):
            return ctx.enter_context(nc.semaphore(name))

        bank = [ctx.enter_context(nc.psum_tensor(f"bank{i}", [P, 512], f32)) for i in range(8)]

        rows_d = nc.dram_tensor("rows_d", [N, 2 * D], f16, kind="Internal").ap()
        x1_d = nc.dram_tensor("x1_d", [N, D], f32, kind="Internal").ap()
        rows_v = rows_d.rearrange("(t p) c -> p t c", p=P)
        x1_v = x1_d.rearrange("(t p) d -> p t d", p=P)

        xs = sb("xs", [P, NT, D], f32)
        flat = xs[:, :, :].rearrange("p t d -> p (t d)")
        hcols = FT * C
        hid = flat[:, 0:hcols].bitcast(f16).rearrange("p (a f c) -> p a f c", a=2, f=FT)
        stage = flat[:, hcols:hcols + ST * D].rearrange("p (s d) -> p s d", s=ST)
        rows = sb("rows", [P, 2, G4, 2 * D], f16)
        xn = sb("xn", [P, 2, G4, D], f32)
        xt2 = sb("xt2", [P, 2, 2, 2 * KD, P], f16)
        bst = sb("bst", [P, 2, G4, 6], f32)
        mv = sb("mv", [P, 2, G4, 2], f32)
        rstd = sb("rstd", [P, 2, G4], f32)
        nmean = sb("nmean", [P, 2, G4], f32)
        ident16 = sb("ident16", [P, P], f16)
        ident = sb("ident", [P, P], f32)
        sel8 = sb("sel8", [P, E], f32)
        same_e = sb("same_e", [P, P], f32)
        before_e = sb("before_e", [P, P], f32)
        edesc = sb("edesc", [P, E], f32)
        mhalf = sb("mhalf", [P, G4], f32)
        slot_a = sb("slot_a", [P, P, LT], b16)
        slot_b = sb("slot_b", [P, ST], f32)
        digit_f = sb("digit_f", [P, ROUNDS + 1], f32)
        cand_f = sb("cand_f", [P, ROUNDS + 1, 4], f32)
        cand_i = sb("cand_i", [P, ROUNDS + 1, 4], i32)
        rw8 = sb("rw8", [E, D], f32)
        rwa = sb("rwa", [P, 2], f32)
        rws = sb("rws", [P, 8], f32)
        rwh = sb("rwh", [E, 2, D], f16)
        rwT = sb("rwT", [P, 2, KD, E], f16)
        lg = sb("lg", [P, NT, E], f32)
        t1 = sb("t1", [P, NT, E], f32)
        t2 = sb("t2", [P, NT, E], f32)
        t3 = sb("t3", [P, NT, E], f32)
        v1 = sb("v1", [P, NT], f32)
        v2 = sb("v2", [P, NT], f32)
        wT = sb("wT", [P, 4 * P], f32)
        kT = sb("kT", [P, 4 * P], f32)
        rT = sb("rT", [P, 4 * P], f32)
        cand = sb("cand", [P, 3, 4], i32)
        flags = sb("flags", [P, 3], f32)
        digit = sb("digit", [P, 1], f32)
        digit_at = sb("digit_at", [P, 1], i32)
        cnt = sb("cnt", [P, 3], f32)
        am4 = sb("am4", [P, 3, 4], f32)
        sc_all = sb("sc_all", [P, E, 6], f32)
        tot = sb("tot", [P, 4], f32)
        pos_a = sb("pos_a", [P, E, NT], b16)
        pos_b = sb("pos_b", [P, E, NT], b16)
        val = sb("val", [P, E, NT, 5], b16)
        hot_a = sb("hot_a", [P, 2, P, LT], b16)
        hot_b = sb("hot_b", [P, 2, LT, ST], b16)
        hot_v = sb("hot_v", [P, 2, LT, 5, ST], b16)
        id_next = sb("id_next", [P, ST], u32)
        id_cur = sb("id_cur", [P, ST], u32)
        w_next = sb("w_next", [P, ST], f32)
        w_tmp = sb("w_tmp", [P, ST], f32)
        w_fac = sb("w_fac", [P, ST], f32)
        lst = sb("lst", [P, 5 * ST], f32)
        v3 = sb("v3", [P, NT], f32)
        v4 = sb("v4", [P, NT], f32)
        raw_gu = sb("raw_gu", [P, 2, KD * F], f32)
        raw_d = sb("raw_d", [P, KD * F], f32)
        raw = [raw_gu[:, 0, :], raw_gu[:, 1, :], raw_d[:, :]]
        wgu = [sb(f"w16_{m}", [P, 2, KD, F], f16) for m in "gu"]
        wdn = sb("w16_d", [P, 2, FT, D], f16)
        am = sb("am", [P, 3], f32)
        amr = sb("amr", [P, 3], f32)
        sc_next = sb("sc_next", [P, 6], f32)
        sc_cur = sb("sc_cur", [P, 6], f32)
        gat = sb("gat", [P, ST, 2 * D], f16)
        xT = sb("xT", [P, 2 * KD, C], f16)
        unit_buf = sb("unit_buf", [P, G4 * 2 * D], f32)
        reached = xn[:, 0, 0:2, :].rearrange("p t d -> p (t d)")
        act_s = unit_buf[:, 0:2 * CW].rearrange("p (b c) -> p b c", b=2)
        h32 = unit_buf[:, 2 * CW:(2 + HB) * CW].rearrange("p (b c) -> p b c", b=HB)
        wq32 = sb("wq32", [P, KD, D], f32)
        wv32 = sb("wv32", [P, KD, D], f32)
        wo32 = sb("wo32", [P, KD, D], f32)
        wq16 = sb("wq16", [P, 2, KD, D], f16)
        bq32 = sb("bq32", [2, D], f32)
        bq_part = kT[0:2, KD * P:KD * P + D].bitcast(f16).rearrange("p (a d) -> p a d", a=2)
        bq16 = sb("bq16", [2, D], f16)
        bq_max = sb("bq_max", [2, 1], f32)
        bq_one = sb("bq_one", [2, P], f16)
        bo_b = sb("bo_b", [P, D], f32)
        bv_p = sb("bv_p", [P, KD], f32)
        same_h = sb("same_h", [P, P], f32)
        sel_h = sb("sel_h", [P, P // DH], f32)
        ones = sb("ones", [P, 1], f16)
        qb = gat[:, :, :].rearrange("p s c -> p (s c)")[:, 0:4 * G4 * D].bitcast(f32).rearrange(
            "p (b t d) -> p b t d", b=2, t=G4)
        ekb = xT[:, :, :].rearrange("p k c -> p (k c)")[:, 0:4 * G4 * D].bitcast(f32).rearrange(
            "p (b t d) -> p b t d", b=2, t=G4)
        qrow = unit_buf[:, :].bitcast(f16).rearrange("p (b t c) -> p b t c", b=2, t=G4)
        ekrow = wdn[:, :, :, :].rearrange("p a f d -> p (a f d)").rearrange("p (b t c) -> p b t c", b=2, t=G4)
        qT = raw_gu[:, :, :].rearrange("p m c -> p (m c)").bitcast(f16).rearrange(
            "p (t c n) -> p t c n", t=BT, c=2 * KD)
        qmax, qsum = v1[:, :], v3[:, :]
        gt_s = t2[:, :, :].rearrange("p t e -> p (t e)").rearrange("p (k d) -> p k d", k=KD)
        m2f = t3[:, :, :].rearrange("p t e -> p (t e)").rearrange("p (k d) -> p k d", k=KD)
        bvo = rT[:, :].rearrange("p (k d) -> p k d", k=KD)
        ctm = wT[:, 0:KD * P].rearrange("p (k d) -> p k d", k=KD)
        mbv = kT[:, 0:KD * P].rearrange("p (k d) -> p k d", k=KD)
        m2h = kT[:, :].bitcast(f16).rearrange("p (a k d) -> p a k d", a=2, k=KD)
        zr = sb("zr", [P, KD], f32)
        mx2 = sb("mx2", [P, 5], f32)

        s_const = sem("constants_ready")
        s_rwld = sem("router_loaded")
        s_boot = sem("boot_steps_dve")
        s_bootp = sem("boot_steps_pool")
        s_boota = sem("boot_steps_act")
        s_bootpe = sem("boot_steps_pe")
        s_gstep = sem("pool_const_steps")
        s_bootx = sem("boot_scale_steps")
        s_passed = sem("waits_passed")
        s_atw = sem("attention_loaded")

        def ffn_sems(p):
            names = ("loaded kept stat_ready rstd_ready xn_ready hi_ready lo_ready stored0 stored1 turned turned_ok cent_ready "
                     "logit_ready logit_out dstep ex_ready w_ready wt_turned counted compared ranked offset_ready "
                     "third_ready third_counted slots_ready back_turned hot_a_ready hot_b_ready hot_v_ready piece_used ids_ready "
                     "raw_g raw_u raw_d amax_ready amax_all scales_ready gu_hi gu_lo d_hi d_lo cur_ready "
                     "g_ready u_ready s_ready h32_ready hhi_ready h_ready d_ready d_out landed added "
                     "wfac_ready pstep").split()
            first = E * "ab".index(p)
            scaled = "ab".index(p)
            only_first = ("loaded", "amax_ready", "amax_all")
            return namedtuple("FfnSems", names + ["first", "scaled"])(
                *(None if scaled and n in only_first else sem(f"{n}_{p}") for n in names), first, scaled)

        class Chain:

            def __init__(self, eng, sm):
                self.eng, self.sm, self.base, self.n = eng, sm, 0, 0

            def mark(self, ins):
                self.n += 1
                return ins.then_inc(self.sm, 1)

            def wait(self):
                self.eng.wait_ge(self.sm, self.base + self.n)

            def step(self, ins):
                self.mark(ins)
                self.wait()

            def enter(self, i, per):
                self.start, self.per = self.base + self.n, per
                self.base, self.n = self.start + i * per, 0

            def leave(self, trips):
                assert self.n == self.per, (self.n, self.per)
                self.base, self.n = self.start + trips * self.per, 0

        gathered = [sem(f"gathered{j}") for j in range(ST // 2)]
        turned = [sem(f"rows_turned{j}") for j in range(ST // 2)]
        sems = [ffn_sems("a"), ffn_sems("b")]
        at_names = ("x1_in stat rstd xn hi lo q cent ex qs qhi qlo ekhi eklo gt gt_out "
                    "out x2 ctx ctm a m_amax m_max m_scale m_hi m_lo dstep").split()
        at = namedtuple("AttentionSems", at_names)(*(sem(f"at_{n}") for n in at_names))
        x1_first = sem("at_x1_first")
        xt_in = [sem(f"at_rows_turned{r}") for r in range(2)]
        qt_in = [sem(f"at_queries_turned{r}") for r in range(2)]
        block = ctx.enter_context(nc.Block())
        bank16 = [b[:, :].bitcast(f16) for b in bank]

        def settle(eng):
            eng.sem_inc(s_passed, 1)

        def scales(ch, v, a, s, inv):
            ch.step(v.tensor_scalar_max(s, a, 2.0 ** -20))
            ch.step(v.tensor_scalar(s.bitcast(i32), s.bitcast(i32), 0x7F800000, None, ALU.bitwise_and))
            ch.step(v.tensor_scalar(s.bitcast(i32), s.bitcast(i32), -1.0, float((254 + WTOP) * ONE), mult, add))
            ch.step(v.tensor_scalar(inv.bitcast(i32), s.bitcast(i32), -1.0, float(254 * ONE), mult, add))

        def raw_src(n):
            pick = (lambda w: w[n:n + 1, :, :]) if isinstance(n, int) else (lambda w: w[bass.ds(n, 1), :, :])
            return [pick(wg).rearrange("o (k p) f -> p (o k) f", p=P),
                    pick(wu).rearrange("o (k p) f -> p (o k) f", p=P),
                    pick(wd).rearrange("o (j p) d -> p (o j) d", p=P)]

        raw_dst = [raw[0].rearrange("p (k f) -> p k f", k=KD),
                   raw[1].rearrange("p (k f) -> p k f", k=KD),
                   raw[2].rearrange("p (j d) -> p j d", j=FT)]

        def halves(m, h):
            if m < 2:
                r = raw_dst[m][:, :, h * F // 2:(h + 1) * F // 2]
                w = wgu[m][:, :, :, h * F // 2:(h + 1) * F // 2]
            else:
                r = raw_dst[2][:, h * FT // 2:(h + 1) * FT // 2, :]
                w = wdn[:, :, h * FT // 2:(h + 1) * FT // 2, :]
            return r, w[:, 0], w[:, 1]

        RMAX = bass.bass_isa.ReduceOp.max

        def bc(ap, axis, n):
            ap = ap.unsqueeze(axis)
            shape = list(ap.shape)
            shape[axis] = n
            return ap.to_broadcast(shape)

        def col(ap, i, n=1):
            return ap[:, i:i + n] if isinstance(i, int) else ap[:, bass.ds(i, n)]

        def wait_for(eng, sm, n):
            if not (isinstance(n, int) and n <= 0):
                eng.wait_ge(sm, n)

        def tiles(ap, t, n):
            return ap[:, t:t + n] if isinstance(t, int) else ap[:, bass.ds(t, n)]

        def batches(eng, body):
            body(-1, range(QUADS))
            body(0, range(QUADS))
            with eng.Fori(0, B - 2) as i:
                body(i + 1, range(QUADS))
            body(B - 1, range(QUADS - 1))

        def quad(b, j):
            b, j = b + j // QUADS, j % QUADS
            return None if isinstance(b, int) and not 0 <= b < B else (b, j)

        def quads(b, j):
            s = j + 1
            return [quad(b, s + n) for n in (3, 2, 1, 0, -1, -1 - QUADS)]

        def nothing(n):
            pass

        def route_part(ap, h):
            return ap[:, 0:PAIR * FIRST] if h == 0 else ap[:, PAIR * FIRST:NT]

        def in_batches(b):
            return not isinstance(b, int) or 0 <= b < B

        at_rows = [rows[:, 0], rows[:, 1]]
        spare_w = wgu[0][:, :, :, :].rearrange("p a k f -> p (a k f)").rearrange("p (b t c) -> p b t c", b=2, t=G4)
        at_rows += [spare_w[:, 0], spare_w[:, 1]]
        at_xt = [xt2[:, :, :, :, :].rearrange("p h t c n -> p (h t) c n"),
                 wgu[1][:, :, :, :].rearrange("p a k f -> p (a k f)")[:, 0:G4 * 2 * D].rearrange(
                     "p (t c n) -> p t c n", t=G4, c=2 * KD)]

        def turned_by(q):
            b, j = q
            return 16 * (QUADS // 2 * b + j // 2 + 1)

        xt2_flat = xt2[:, :, :, :, :].rearrange("p h t c n -> p h (t c n)")
        FIRST = STEPS - 2
        TURN_BANK = (0, 3)
        AMAX_AT = {7 + 2 * k: (k // 4, k % 4) for k in range(12)}
        PIECE_AT = {6 + 2 * i: i for i in range(LP)}
        PE_PIECE_AT = {u + 3: i for u, i in PIECE_AT.items()}

        @block.gpsimd
        def _(pool):
            gs = Chain(pool, s_gstep)
            gs.mark(pool.memset(ident[:, :], 0.0))
            gs.step(pool.memset(ident16[:, :], 0.0))
            for m in (ident, ident16):
                gs.mark(pool.affine_select(out=m[:, :], in_=m[:, :], compare_op=ALU.not_equal, fill=1.0, base=0,
                                           pattern=[[-1, P]], channel_multiplier=1))
            for S in sems:
                for sm, n in ((S.stored0, 16), (S.stored1, 16), (S.turned_ok, 2), (S.lo_ready, 2), (S.logit_out, 1),
                              (S.s_ready, 2), (S.h32_ready, 2), (S.h_ready, HB), (S.d_out, 2), (S.d_ready, 1),
                              (S.piece_used, 2)):
                    pool.sem_inc(sm, n)
            pool.sem_inc(at.x2, 2)
            small = dict(allow_small_or_imprecise_dtypes=True)
            gs.mark(pool.iota(edesc[:, :], [[-1, E]], base=E, channel_multiplier=0, **small))
            gs.step(pool.memset(mhalf[:, :], -0.5))
            pool.wait_ge(s_boot, 4)
            pool.partition_all_reduce(rws[:, 4:6], rwa[:, :], P, RMAX).then_inc(s_bootp, 1)

            def routing_constants():
                gs.mark(pool.iota(slot_a[:, :, :], [[1, P], [0, LT]], base=0, channel_multiplier=0, **small))
                gs.mark(pool.iota(slot_b[:, :], [[1, ST]], base=1, channel_multiplier=0, **small))
                gs.mark(pool.iota(val[:, :, :, 0], [[0, E], [1, NT]], base=0, channel_multiplier=0, **small))
                gs.mark(pool.iota(val[:, :, :, 1], [[0, E], [0, NT]], base=0, channel_multiplier=1, **small))
                for r in range(ROUNDS):
                    gs.mark(pool.memset(digit_f[:, r:r + 1], 4.0 ** (ROUNDS - 1 - r)))
                gs.mark(pool.memset(digit_f[:, ROUNDS:], 0.0))
                gs.step(pool.iota(cand_f[:, :, :], [[0, ROUNDS + 1], [1, 4]], base=0, channel_multiplier=0, **small))
                gs.step(pool.tensor_tensor(cand_f[:, :, :], cand_f[:, :, :], bc(digit_f[:, :], 2, 4), mult))
                gs.mark(pool.tensor_copy(cand_i[:, :, :], cand_f[:, :, :]))
                gs.step(pool.affine_select(out=before_e[:, :], in_=same_e[:, :], compare_op=ALU.is_gt, fill=0.0, base=0,
                                           pattern=[[1, P]], channel_multiplier=-1))
                pool.sem_inc(s_const, 1)

            def weight_max(S, n):
                pool.wait_ge(S.amax_ready, n + 1)
                settle(pool)
                pool.partition_all_reduce(amr[:, :], am[:, :], P, RMAX).then_inc(S.amax_all, 1)

            def list_piece(S, n, i):
                r, at = i % 2, slice(i * LT, (i + 1) * LT)
                vv = col(val[:, :, at, :], n)[:, 0]
                pool.wait_ge(S.hot_b_ready, LP * n + i + 1)
                pool.tensor_tensor(hot_v[:, r], bc(hot_b[:, r], 2, 5), bc(vv, 3, ST), mult).then_inc(S.hot_v_ready, 1)

            def gather(S, n):
                pool.wait_ge(S.ids_ready, n + 1)
                settle(pool)
                for s in range(ST):
                    pool.indirect_dma_start(
                        out=gat[:, s, :], out_offset=None, in_=rows_d,
                        in_offset=bass.IndirectOffsetOnAxis(ap=id_next[:, s:s + 1], axis=0),
                        bounds_check=N - 1).then_inc(gathered[s // 2], 16)

            def expert(S, e, dst, last):
                if not last:
                    for i in range(LP):
                        list_piece(S, e + 1, i)
                    if not S.scaled:
                        weight_max(S, e + 1)
                    gather(S, e + 1)
                for s in range(ST):
                    pool.wait_ge(S.d_out, ST * e + s + 1 + 2)
                    settle(pool)
                    pool.indirect_dma_start(
                        out=dst, out_offset=bass.IndirectOffsetOnAxis(ap=id_cur[:, s:s + 1], axis=0),
                        in_=stage[:, s, :], in_offset=None, bounds_check=N - 1, compute_op=add).then_inc(S.added, 16)
                pool.wait_ge(S.added, 16 * ST * e + 16 * ST)
                pool.sem_inc(S.landed, 1)

            def ffn(S, dst, head, beside):
                def power(q, r):
                    pool.wait_ge(S.stat_ready, q + 1)
                    pool.tensor_tensor(rstd[:, r, :], rstd[:, r, :], mhalf[:, :], ALU.pow).then_inc(S.rstd_ready, 1)

                def low(q, r):
                    pool.wait_ge(S.hi_ready, q + 1)
                    pool.tensor_tensor(rows[:, r, :, D:2 * D], xn[:, r, :, :], rows[:, r, :, 0:D],
                                       sub).then_inc(S.lo_ready, 1)

                def step(i, beside):
                    power(2 * i + 1, 1)
                    low(2 * i, 0)
                    beside(2 * i)
                    power(2 * i + 2, 0)
                    low(2 * i + 1, 1)
                    beside(2 * i + 1)

                power(0, 0)
                beside(-1)
                for i in range(head):
                    step(i, beside)
                with pool.Fori(head, STEPS - 1) as i:
                    step(i, nothing)
                power(2 * STEPS - 1, 1)
                low(2 * STEPS - 2, 0)
                low(2 * STEPS - 1, 1)
                if not S.scaled:
                    routing_constants()
                ch = Chain(pool, S.pstep)
                parts = [val[:, :, :, 2 + k].rearrange("p e t -> p t e") for k in range(3)]
                pool.wait_ge(S.w_ready, 2)
                ch.step(pool.tensor_tensor(t3[:, :, :], t1[:, :, :], t2[:, :, :], mult))
                ch.step(pool.tensor_copy(parts[0], t3[:, :, :]))
                ch.step(pool.tensor_tensor(lg[:, :, :], t3[:, :, :], parts[0], sub))
                ch.step(pool.tensor_copy(parts[1], lg[:, :, :]))
                ch.step(pool.tensor_tensor(parts[2], lg[:, :, :], parts[1], sub))
                if not S.scaled:
                    weight_max(S, 0)
                for i in range(LP):
                    list_piece(S, 0, i)
                for stored in (S.stored0, S.stored1):
                    pool.wait_ge(stored, 16 + 16 * STEPS)
                gather(S, 0)
                pool.wait_ge(S.kept, 16 * (1 if S is sems[0] else B * QUADS))
                pool.sem_inc(S.landed, 1)
                with pool.Fori(0, E - 1) as e:
                    expert(S, e, dst, False)
                expert(S, E - 1, dst, True)

            def power(b, j):
                q, r = QUADS * b + j, j % 2
                pool.wait_ge(at.stat, q + 1)
                pool.tensor_tensor(rstd[:, r, :], rstd[:, r, :], mhalf[:, :], ALU.pow).then_inc(at.rstd, 1)
                pool.wait_ge(at.rstd, 2 * q + 1)
                pool.tensor_tensor(nmean[:, r, :], nmean[:, r, :], rstd[:, r, :], mult).then_inc(at.rstd, 1)

            def norm_low(b, j):
                pool.wait_ge(at.hi, QUADS * b + j + 1)
                pool.tensor_tensor(at_rows[j][:, :, D:2 * D], xn[:, j % 2, :, :], at_rows[j][:, :, 0:D],
                                   sub).then_inc(at.lo, 1)

            def queries_low(b, j):
                pool.wait_ge(at.qhi, QUADS * b + j + 1)
                pool.tensor_tensor(qrow[:, j % 2, :, D:2 * D], qb[:, j % 2], qrow[:, j % 2, :, 0:D],
                                   sub).then_inc(at.qlo, 1)

            def keys_low(b, j):
                pool.wait_ge(at.ekhi, QUADS * b + j + 1)
                pool.tensor_tensor(ekrow[:, j % 2, :, D:2 * D], ekb[:, j % 2], ekrow[:, j % 2, :, 0:D],
                                   sub).then_inc(at.eklo, 1)

            def m2_max(m):
                pool.wait_ge(at.m_amax, m + 1)
                settle(pool)
                pool.partition_all_reduce(mx2[:, 1:2], mx2[:, 0:1], P, RMAX).then_inc(at.m_max, 1)

            def body(b, steps):
                for j in steps:
                    far, ahead, _, now, _, _ = quads(b, j)
                    if ahead:
                        norm_low(*ahead)
                    if j == 0 and in_batches(b - 1):
                        m2_max(b - 1)
                    if far:
                        power(*far)
                    if now:
                        keys_low(*now)
                        queries_low(*now)

            def attention_end(n):
                if n == 2:
                    m2_max(B - 1)

            ffn(sems[0], x1_d, 0, nothing)
            batches(pool, body)
            ffn(sems[1], of, 4, attention_end)

        @block.sync
        def _(sp):
            sp.dma_start(rw8[:, :], router_w).then_inc(s_rwld, 16)
            sp.dma_start(wq32[:, :, :], wq.rearrange("(k p) d -> p k d", p=P)).then_inc(s_rwld, 16)
            sp.dma_start(bq32[:, :], bq.unsqueeze(0).to_broadcast([2, D])).then_inc(s_rwld, 16)

            def pair(ap, i):
                return col(ap, i * PAIR, PAIR)

            def store_rows(S, i):
                for b in range(2):
                    sp.wait_ge(S.lo_ready, 2 * i + b + 1 + 2)
                    sp.dma_start(col(rows_v, i * PAIR + b * G4, G4), rows[:, b, :, :]).then_inc((S.stored0, S.stored1)[b], 16)

            def load_x(loaded, src_v, i):
                sp.dma_start(pair(xs, i), pair(src_v, i)).then_inc(loaded, 16)

            def load_quad(loaded, src_v, q):
                sp.dma_start(col(xs, q * G4, G4), col(src_v, q * G4, G4)).then_inc(loaded, 16)

            def ffn_in(S, src_v):
                load_quad(S.loaded, src_v, 0)
                sp.wait_ge(S.loaded, 16)
                load_quad(S.loaded, src_v, 1)
                sp.wait_ge(S.loaded, 32)
                load_x(S.loaded, src_v, 1)
                with sp.Fori(0, STEPS - 2) as i:
                    sp.wait_ge(S.loaded, 16 * i + 48)
                    load_x(S.loaded, src_v, i + 2)
                    store_rows(S, i)
                store_rows(S, STEPS - 2)
                store_rows(S, STEPS - 1)
                first_raw(S)

            def first_raw(S):
                for dst, src, loaded in zip(raw_dst, raw_src(0), (S.raw_g, S.raw_u, S.raw_d)):
                    sp.dma_start(dst, src).then_inc(loaded, 16)

            def load_raw(S, n):
                src = raw_src(n)
                sp.wait_ge(gathered[ST // 2 - 1], 32 * (n + S.first))
                settle(sp)
                for m, (loaded, split) in enumerate(((S.raw_g, S.gu_lo), (S.raw_u, S.gu_lo), (S.raw_d, S.d_lo))):
                    sp.wait_ge(split, n * (4 if m < 2 else 2))
                    sp.dma_start(raw_dst[m], src[m]).then_inc(loaded, 16)

            def turn_rows(S, n):
                for s in range(ST):
                    if s % 2 == 0:
                        sp.wait_ge(gathered[s // 2], 32 * (n + S.first) + 32)
                        settle(sp)
                    sp.dma_start_transpose(xT[:, :, s * P:(s + 1) * P], gat[:, s, :]).then_inc(turned[s // 2], 16)

            def experts(S):
                turn_rows(S, 0)
                with sp.Fori(0, E - 1) as e:
                    load_raw(S, e + 1)
                    sp.wait_ge(S.u_ready, UNITS * e + UNITS)
                    settle(sp)
                    turn_rows(S, e + 1)
                sp.wait_ge(S.landed, E + 1)

            ffn_in(sems[0], x_v)
            sp.dma_start(x1_v, xs[:, :, :]).then_inc(sems[0].kept, 16)
            for dst, src in ((wv32[:, :, :], wv.rearrange("(k p) d -> p k d", p=P)),
                             (wo32[:, :, :], wo.rearrange("(k p) d -> p k d", p=P)),
                             (bo_b[:, :], bo.unsqueeze(0).to_broadcast([P, D]))):
                sp.dma_start(dst, src).then_inc(s_atw, 16)
            sp.dma_start(bv_p[:, :], bv.rearrange("(k p) -> p k", p=P), allow_slow_non_contiguous=True).then_inc(s_atw, 16)
            experts(sems[0])
            def load_quads(n, q, quads):
                wait_for(sp, at.x1_in, 16 * n)
                sp.dma_start(xs[:, q * G4:(q + quads) * G4], x1_v[:, q * G4:(q + quads) * G4]).then_inc(at.x1_in, 16)

            def keep(q):
                sp.wait_ge(at.x2, 2 * q + 2 + 2)
                settle(sp)
                sp.dma_start(col(o_v, q * G4, G4), col(xs, q * G4, G4)).then_inc(sems[1].kept, 16)

            def turn_x(b, j):
                q = QUADS * b + j
                sp.wait_ge(at.lo, q + 1)
                settle(sp)
                wait_for(sp, at.q, 2 * (q - 1))
                settle(sp)
                sp.dma_start_transpose(at_xt[j % 2].rearrange("p t c n -> p (t c) n"),
                                       at_rows[j].rearrange("p t c -> p (t c)")).then_inc(xt_in[j % 2], 16)

            def turn_q(b, j):
                q = QUADS * b + j
                sp.wait_ge(at.qlo, q + 1)
                settle(sp)
                wait_for(sp, at.out, 2 * (q + 1 - QUADS))
                settle(sp)
                sp.dma_start_transpose(qT[:, G4 * j:G4 * (j + 1)].rearrange("p t c n -> p (t c) n"),
                                       qrow[:, j % 2].rearrange("p t c -> p (t c)")).then_inc(qt_in[j % 2], 16)

            def body(b, steps):
                for j in steps:
                    _, ahead, _, _, past, done = quads(b, j)
                    late = not (isinstance(b, int) and b == 0) and j < 2
                    if past and not late:
                        turn_q(*past)
                    if past and late and j == 1:
                        turn_q(b, 0)
                    if ahead:
                        turn_x(*ahead)
                    if past and late and j == 1:
                        turn_q(*past)
                    if done and j:
                        keep(QUADS * done[0] + j - 1)
                        if j == QUADS - 1:
                            keep(QUADS * done[0] + j)
                    if isinstance(b, int) and b == -1:
                        load_quads(j, QUADS + j, 1)
                    if isinstance(b, int) and b == 0:
                        load_quads(QUADS + j, 2 * QUADS + j * (B - 2), B - 2)

            for j in range(2):
                load_quad(x1_first, x1_v, j)
                sp.wait_ge(x1_first, 16 * j + 16)
            sp.dma_start(xs[:, 2 * G4:BT], x1_v[:, 2 * G4:BT]).then_inc(x1_first, 16)
            batches(sp, body)

            last = (B - 1) * QUADS
            turn_q(B - 1, QUADS - 1)
            keep(last - 2)
            keep(last - 1)
            for i in range(3):
                store_rows(sems[1], i)
            keep(last)
            keep(last + 1)
            store_rows(sems[1], 3)
            keep(last + 2)
            store_rows(sems[1], 4)
            keep(last + 3)
            with sp.Fori(5, STEPS) as i:
                store_rows(sems[1], i)
            sp.wait_ge(at.out, 2 * B * QUADS)
            first_raw(sems[1])
            experts(sems[1])

        @block.scalar
        def _(act):
            def split_hi(m, h, done):
                r, hi, _ = halves(m, h)
                act.activation(hi, r, ACT.Copy, scale=sc_next[:, m:m + 1] if m < 2 else sc_cur[:, 2:3]).then_inc(done, 1)

            def ffn_in(S, head, beside):
                def high(i, r):
                    act.wait_ge((S.stored0, S.stored1)[r], 16 * i + 16)
                    act.wait_ge(S.xn_ready, 2 * i + r + 1)
                    act.activation(rows[:, r, :, 0:D], xn[:, r, :, :], ACT.Copy).then_inc(S.hi_ready, 1)

                def turned(q):
                    for k in range(2):
                        act.wait_ge(S.turned, 2 * q + k + 1)
                        wait_for(act, S.logit_ready, 2 * q + k - 1)
                        act.activation(xt2_flat[:, k, :], bank16[TURN_BANK[k]], ACT.Copy).then_inc(S.turned_ok, 1)

                def logits_out(i):
                    act.wait_ge(S.logit_ready, 4 * i + 4)
                    act.activation(col(lg, PAIR * i, PAIR).rearrange("p t e -> p (t e)"), bank[2][:, 0:PAIR * E], ACT.Copy,
                                   scale=rws[:, 6:7]).then_inc(S.logit_out, 1)

                def step(i, beside):
                    high(i, 0)
                    turned(2 * i - 1)
                    logits_out(i - 1)
                    beside(2 * i)
                    high(i, 1)
                    turned(2 * i)
                    beside(2 * i + 1)

                def exponentials(h):
                    act.wait_ge(S.cent_ready, h + 1)
                    act.activation(route_part(t1, h), route_part(lg, h), ACT.Exp).then_inc(S.ex_ready, 1)

                high(0, 0)
                beside(-1)
                high(0, 1)
                beside(0)
                turned(0)
                beside(1)
                for i in range(1, 1 + head):
                    step(i, beside)
                with act.Fori(1 + head, STEPS - 1) as i:
                    step(i, nothing)
                high(STEPS - 1, 0)
                turned(2 * STEPS - 3)
                logits_out(STEPS - 2)
                high(STEPS - 1, 1)
                exponentials(0)
                turned(2 * STEPS - 2)
                turned(2 * STEPS - 1)
                logits_out(STEPS - 1)
                exponentials(1)
                with act.Fori(0, ROUNDS) as r:
                    act.wait_ge(S.third_ready, r + 1)
                    act.activation(xn[:, 0, 2:4, :].rearrange("p t d -> p (t d)"), reached, ACT.Copy,
                                   accum_out=cnt[:, 2:3]).then_inc(S.third_counted, 1)

            def unit_silu(S, e, u):
                act.wait_ge(S.g_ready, UNITS * e + u + 1)
                act.wait_ge(S.h32_ready, UNITS * e + u + 1)
                act.activation(act_s[:, u % 2, :], bank[u % 2][:, 0:CW], ACT.Silu,
                               scale=sc_cur[:, 3:4]).then_inc(S.s_ready, 1)

            def unit_hi(S, e, u):
                f, c = divmod(u, CH)
                act.wait_ge(S.h32_ready, UNITS * e + u + 1 + 2)
                act.activation(hid[:, 0, f, c * CW:(c + 1) * CW], h32[:, u % HB, :], ACT.Copy).then_inc(S.hhi_ready, 1)

            def expert(S, e, last):
                act.wait_ge(S.cur_ready, e + 1)
                for u in range(UNITS):
                    unit_silu(S, e, u)
                    if u:
                        unit_hi(S, e, u - 1)
                    if u in (1, 3):
                        if u == 1:
                            act.wait_ge(S.raw_d, 16 * e + 16)
                            act.wait_ge(S.d_ready, ST * e + 1)
                        split_hi(2, u // 2, S.d_hi)
                unit_hi(S, e, UNITS - 1)
                for s in range(ST):
                    act.wait_ge(S.d_ready, ST * e + s + 1 + 1)
                    if s == 0:
                        act.wait_ge(S.landed, e + 1)
                        act.wait_ge(S.wfac_ready, e + 1)
                    act.activation(stage[:, s, :], bank[4 + s % 2][:, 0:D], ACT.Copy,
                                   scale=w_fac[:, s:s + 1]).then_inc(S.d_out, 1)
                    if not last and s < 4:
                        if s == 0:
                            act.wait_ge(S.scales_ready, e + 2)
                        if s < 2:
                            act.wait_ge((S.raw_g, S.raw_u)[s], 16 * e + 32)
                        split_hi(s % 2, s // 2, S.gu_hi)

            def ffn(S, head, beside):
                if S is sems[0]:
                    act.wait_ge(s_boot, 5)
                    act.activation(rwh[:, 0, :], rw8[:, :], ACT.Copy, scale=rws[0:E, 0:1]).then_inc(s_boota, 1)
                else:
                    act.wait_ge(at.gt, B * QUADS - 2)
                    act.wait_ge(at.q, 2 * B * QUADS)
                ffn_in(S, head, beside)
                act.wait_ge(S.scales_ready, 1)
                for loaded in (S.raw_g, S.raw_u):
                    act.wait_ge(loaded, 16)
                for k in range(4):
                    split_hi(k % 2, k // 2, S.gu_hi)
                act.wait_ge(S.kept, 16 * (1 if S is sems[0] else B * QUADS))
                with act.Fori(0, E - 1) as e:
                    expert(S, e, False)
                expert(S, E - 1, True)

            def norm_x(b, j):
                q, r = QUADS * b + j, j % 2
                act.wait_ge(at.rstd, 2 * q + 2)
                wait_for(act, at.lo, q - 1)
                for g in range(G4):
                    last = act.activation(xn[:, r, g, :], tiles(xs, G4 * q + g, 1)[:, 0], ACT.Identity,
                                          scale=rstd[:, r, g:g + 1], bias=nmean[:, r, g:g + 1])
                last.then_inc(at.xn, 1)

            def norm_hi(b, j):
                q, r = QUADS * b + j, j % 2
                act.wait_ge(at.xn, q + 1)
                wait_for(act, at.gt, q - 3)
                act.activation(at_rows[j][:, :, 0:D], xn[:, r, :, :], ACT.Copy).then_inc(at.hi, 1)

            def queries_exp(b, j):
                act.wait_ge(at.cent, QUADS * b + j + 1)
                act.activation(qb[:, j % 2], qb[:, j % 2], ACT.Exp, scale=rws[:, 7:8]).then_inc(at.ex, 1)

            def keys_exp(b, j):
                q, r = QUADS * b + j, j % 2
                act.wait_ge(at.qs, q + 1)
                wait_for(act, at.eklo, q - 1)
                wait_for(act, at.gt, q - 1)
                act.activation(ekb[:, r], qb[:, r], ACT.Exp, scale=1.0 / QTOP)
                act.activation(ekrow[:, r, :, 0:D], qb[:, r], ACT.Exp, scale=1.0 / QTOP).then_inc(at.ekhi, 1)

            def queries_hi(b, j):
                q, r = QUADS * b + j, j % 2
                if j >= 2 or not (isinstance(b, int) and b == 0):
                    act.wait_ge(qt_in[r], turned_by((b, j - 2)))
                act.activation(qrow[:, r, :, 0:D], qb[:, r], ACT.Copy).then_inc(at.qhi, 1)

            def m2_hi(m):
                act.wait_ge(at.m_scale, m + 1)
                act.activation(m2h[:, 0], m2f, ACT.Copy, scale=mx2[:, 2:3]).then_inc(at.m_hi, 1)

            def products_out(m):
                act.wait_ge(at.gt, QUADS * (m + 1))
                act.activation(gt_s, bank[4][:, :].rearrange("p (k d) -> p k d", k=KD), ACT.Copy,
                               scale=1.0 / XSCALE).then_inc(at.gt_out, 1)

            def body(b, steps):
                for j in steps:
                    _, ahead, _, now, _, _ = quads(b, j)
                    if ahead:
                        norm_x(*ahead)
                    if now:
                        queries_exp(*now)
                    if ahead:
                        norm_hi(*ahead)
                    if j == 0 and in_batches(b - 1):
                        m2_hi(b - 1)
                    if now:
                        keys_exp(*now)
                    if j == QUADS - 1 and in_batches(b):
                        products_out(b)
                    if now:
                        queries_hi(*now)

            def attention_end(n):
                if n == -1:
                    products_out(B - 1)
                if n == 3:
                    m2_hi(B - 1)

            ffn(sems[0], 0, nothing)
            act.activation(wq16[:, 0, :, :], wq32[:, :, :], ACT.Copy, scale=rws[:, 1:2])
            act.activation(bq_part[:, 0], bq32[:, :], ACT.Copy, scale=rws[0:2, 1:2]).then_inc(s_boota, 1)
            batches(act, body)
            ffn(sems[1], 1, attention_end)

        @block.vector
        def _(dve):
            bs = Chain(dve, s_boot)
            dve.wait_ge(s_gstep, 4)
            bs.step(dve.tensor_reduce(sel8[:, :], ident[:, :].rearrange("p (t e) -> p e t", e=E), AX.X, add))
            bs.step(dve.tensor_copy(same_e[:, :].rearrange("p (t e) -> p t e", e=E), bc(sel8[:, :], 1, TC)))
            bs.step(dve.memset(rwa[:, :], 0.0))
            dve.wait_ge(s_rwld, 16 * 3)
            bx = Chain(dve, s_bootx)
            bx.mark(dve.tensor_reduce(rwa[:, 1:2], wq32[:, :, :].rearrange("p k d -> p (k d)"), AX.X, ALU.max,
                                      apply_absolute_value=True))
            bx.step(dve.tensor_reduce(bq_max[:, :], bq32[:, :], AX.X, ALU.max, apply_absolute_value=True))
            bx.step(dve.tensor_tensor(rwa[0:2, 1:2], rwa[0:2, 1:2], bq_max[:, :], ALU.max))
            bs.step(dve.tensor_reduce(rwa[0:E, 0:1], rw8[:, :], AX.X, ALU.max, apply_absolute_value=True))

            def router(n):
                if n == 0:
                    dve.wait_ge(s_bootp, 1)
                    scales(bx, dve, rws[:, 4:6], rws[:, 0:2], rws[:, 2:4])
                    bs.step(dve.tensor_scalar(rws[:, 6:8], rws[:, 2:4], 1.0 / XSCALE, None, mult))
                if n == 1:
                    dve.wait_ge(s_boota, 1)
                    bs.step(dve.scalar_tensor_tensor(rwh[:, 1, :], rw8[:, :], rws[0:E, 0:1], rwh[:, 0, :], mult, sub))
                if n == 2:
                    dve.wait_ge(s_bootpe, 1)
                    bs.step(dve.tensor_copy(rwT[:, :, :, :].rearrange("p a k e -> p (a k e)"),
                                            bank16[7][:, 0:2 * KD * E]))

            def attention_constants():
                dve.wait_ge(s_boota, 2)
                bs.mark(dve.scalar_tensor_tensor(wq16[:, 1, :, :], wq32[:, :, :], rws[:, 1:2], wq16[:, 0, :, :], mult, sub))
                bs.step(dve.scalar_tensor_tensor(bq_part[:, 1], bq32[:, :], rws[0:2, 1:2], bq_part[:, 0], mult, sub))
                bs.step(dve.tensor_scalar(bq_part[:, 1], bq_part[:, 1], ident[0:2, 1:2], None, mult))
                bs.mark(dve.scalar_tensor_tensor(bq16[:, :], bq_part[:, 0], ident[0:2, 0:1], bq_part[:, 1], mult, add))
                bs.mark(dve.memset(ones[:, :], 1.0))
                bs.mark(dve.memset(bq_one[:, :], XSCALE))
                bs.step(dve.tensor_reduce(sel_h[:, :], ident[:, :].rearrange("p (h d) -> p h d", d=DH), AX.X, add))
                bs.step(dve.tensor_copy(same_h[:, :].rearrange("p (h d) -> p h d", d=DH), bc(sel_h[:, :], 2, DH)))

            def weight_amax(S, m, n, i):
                q = KD * F // 4
                if i == 0:
                    dve.wait_ge((S.raw_g, S.raw_u, S.raw_d)[m], 16 * n + 16)
                ch = dve.tensor_reduce(am4[:, m, i:i + 1], raw[m][:, i * q:(i + 1) * q], AX.X, ALU.max,
                                       apply_absolute_value=True)
                return ch

            def weight_scales(S, ch, n):
                kept = col(sc_all, n)[:, 0]
                if S.scaled:
                    dve.tensor_copy(sc_next[:, :], kept).then_inc(S.scales_ready, 1)
                else:
                    dve.wait_ge(S.amax_all, n + 1)
                    scales(ch, dve, amr[:, :], sc_next[:, 0:3], sc_next[:, 3:6])
                    dve.tensor_copy(kept, sc_next[:, :]).then_inc(S.scales_ready, 1)

            def split_lo(m, h, done):
                r, hi, lo = halves(m, h)
                dve.scalar_tensor_tensor(lo, r, sc_next[:, m:m + 1] if m < 2 else sc_cur[:, 2:3], hi,
                                         mult, sub).then_inc(done, 1)

            def ffn_in(S, ch, wait_x, head, beside):
                def stats(i, r):
                    t = i * PAIR + r * G4
                    wait_x(i, r)
                    for g in range(G4):
                        ch.mark(dve.bn_stats(bst[:, r, g, :], tiles(xs, t + g, 1)[:, 0]))
                    ch.wait()
                    settle(dve)
                    for g in range(G4):
                        ch.mark(dve.bn_aggr(mv[:, r, g, :], bst[:, r, g, :]))
                    ch.wait()
                    dve.tensor_scalar(rstd[:, r, :], mv[:, r, :, 1], EPS, XSCALE ** -2, add, mult).then_inc(S.stat_ready, 1)

                def norm(i, r):
                    t, q = i * PAIR + r * G4, 2 * i + r
                    dve.wait_ge(S.lo_ready, q + 1)
                    dve.wait_ge(S.rstd_ready, q + 1)
                    for g in range(G4):
                        last = dve.tensor_scalar(xn[:, r, g, :], tiles(xs, t + g, 1)[:, 0], mv[:, r, g, 0:1],
                                                 rstd[:, r, g:g + 1], sub, mult)
                    last.then_inc(S.xn_ready, 1)

                def step(i, beside):
                    stats(i, 1)
                    beside(4 * i + 1)
                    norm(i, 0)
                    beside(4 * i + 2)
                    stats(i + 1, 0)
                    beside(4 * i + 3)
                    norm(i, 1)
                    beside(4 * i + 4)

                stats(0, 0)
                beside(0)
                for i in range(head):
                    step(i, beside)
                with dve.Fori(head, STEPS - 1) as i:
                    ch.enter(i - head, 2 * 2 * G4)
                    step(i, nothing)
                    ch.leave(STEPS - 1 - head)
                stats(STEPS - 1, 1)
                norm(STEPS - 1, 0)
                norm(STEPS - 1, 1)

            def route(S, ch):
                def top_two(h):
                    lgs, mask, ex, rest = (route_part(t, h) for t in (lg, t2, t1, t3))
                    m1, m2, m3, m4 = (route_part(t, h) for t in (v1, v2, v3, v4))
                    ed = bc(edesc[:, :], 1, PAIR * (FIRST if h == 0 else STEPS - FIRST))
                    dve.wait_ge(S.logit_out, (FIRST if h == 0 else STEPS) + 1)
                    ch.step(dve.tensor_reduce(m1, lgs, AX.X, ALU.max))
                    dve.tensor_tensor(lgs, lgs, bc(m1, 2, E), sub).then_inc(S.cent_ready, 1)
                    dve.wait_ge(S.cent_ready, h + 1)
                    ch.step(dve.scalar_tensor_tensor(mask, lgs, 0.0, ed, ALU.is_equal, mult))
                    ch.step(dve.tensor_reduce(m2, mask, AX.X, ALU.max))
                    ch.step(dve.tensor_tensor(mask, mask, bc(m2, 2, E), ALU.is_equal))
                    dve.wait_ge(S.ex_ready, h + 1)
                    ch.mark(dve.scalar_tensor_tensor(rest, mask, -2.0, ex, mult, add))
                    ch.step(dve.tensor_reduce(m1, ex, AX.X, add))
                    ch.mark(dve.tensor_reduce(m3, rest, AX.X, ALU.max))
                    ch.step(dve.reciprocal(m1, m1))
                    second = lgs
                    ch.mark(dve.tensor_tensor(second, rest, bc(m3, 2, E), ALU.is_equal))
                    ch.step(dve.scalar_tensor_tensor(m4, m3, 1.0, m1, add, mult))
                    ch.mark(dve.tensor_tensor(second, second, ed, mult))
                    ch.step(dve.tensor_scalar(m4, m4, 1e-6, None, add))
                    ch.mark(dve.tensor_reduce(m2, second, AX.X, ALU.max))
                    ch.step(dve.reciprocal(m4, m4))
                    ch.mark(dve.tensor_tensor(second, second, bc(m2, 2, E), ALU.is_equal))
                    ch.step(dve.tensor_tensor(m1, m1, m4, mult))
                    ch.mark(dve.tensor_tensor(mask, mask, second, add))
                    ch.step(dve.tensor_tensor(ex, ex, bc(m1, 2, E), mult))
                    chunks = slice(0, 2 * FIRST) if h == 0 else slice(2 * FIRST, TC)
                    dve.tensor_tensor(wT[:, :].rearrange("p (g c e) -> p g c e", g=G4, e=E)[:, :, chunks],
                                      ex.rearrange("p (c g) e -> p g c e", g=G4),
                                      mask.rearrange("p (c g) e -> p g c e", g=G4), mult).then_inc(S.w_ready, 1)

                top_two(0)
                top_two(1)
                if not S.scaled:
                    dve.wait_ge(s_const, 1)
                dve.wait_ge(S.wt_turned, 1)
                ch.mark(dve.tensor_copy(wT[:, :], bank[3][:, :]))
                ch.step(dve.tensor_copy(cand[:, 0, :], cand_i[:, 0, :]))
                if not S.scaled:
                    for loaded in (S.raw_g, S.raw_u, S.raw_d):
                        dve.wait_ge(loaded, 16)

                def rounds(i):
                    for k in range(3):
                        r = 3 * i + k
                        dve.tensor_scalar(reached, wT[:, :], cand[:, k, 3:4].bitcast(f32), None,
                                          ALU.is_ge).then_inc(S.third_ready, 1)
                        for j, o in enumerate((kT[:, :], rT[:, :])):
                            c = dve.tensor_scalar(o, wT[:, :], cand[:, k, j + 1:j + 2].bitcast(f32), None, ALU.is_ge, add,
                                                  accum_out=cnt[:, j:j + 1])
                        c.then_inc(S.compared, 1)
                        if not S.scaled and not isinstance(i, int):
                            q = KD * F // 4
                            ch.mark(dve.tensor_reduce(am4[:, k, bass.ds(i, 1)], raw[k][:, bass.ds(i * q, q)], AX.X, ALU.max,
                                                      apply_absolute_value=True))
                        dve.wait_ge(S.counted, r + 1)
                        ch.step(dve.tensor_scalar(flags[:, :], bank[4][:, 0:3], float(C), None, ALU.is_ge, add,
                                                  accum_out=digit[:, :]))
                        ch.step(dve.tensor_scalar(digit_at[:, :], digit[:, :], col(digit_f, r), None, mult))
                        ch.step(dve.scalar_tensor_tensor(cand[:, (k + 1) % 3, :], col(cand_i, r + 1)[:, 0], digit_at[:, :],
                                                         cand[:, k, 0:1].to_broadcast([P, 4]), ALU.bitwise_or,
                                                         ALU.bitwise_or))

                trips = (ROUNDS // 3 - 1) // 2
                with dve.Fori(0, trips) as i:
                    ch.enter(i, 2 * (9 + 3 * (not S.scaled)))
                    rounds(2 * i)
                    rounds(2 * i + 1)
                    ch.leave(trips)
                if not S.scaled:
                    ch.wait()
                    dve.tensor_reduce(am[:, :], am4[:, :, :], AX.X, ALU.max).then_inc(S.amax_ready, 1)
                rounds(ROUNDS // 3 - 1)
                thr = cand[:, 0, 0:1].bitcast(f32)
                ch.mark(dve.tensor_scalar(kT[:, :], wT[:, :], thr, None, ALU.is_gt, add, accum_out=cnt[:, 0:1]))
                dve.tensor_scalar(rT[:, :], wT[:, :], thr, None, ALU.is_equal, add,
                                  accum_out=cnt[:, 1:2]).then_inc(S.ranked, 1)
                dve.wait_ge(S.offset_ready, 1)
                ch.mark(dve.tensor_scalar(tot[:, 0:1], bank[4][:, 0:1], -1.0, float(C), mult, add))
                ch.step(dve.tensor_copy(tot[:, 1:2], bank[4][:, 1:2]))
                ch.step(dve.tensor_tensor_scan(wT[:, :], rT[:, :], rT[:, :], tot[:, 1:2], add, ALU.max))
                ch.step(dve.scalar_tensor_tensor(rT[:, :], wT[:, :], tot[:, 0:1], rT[:, :], ALU.is_le, mult))
                ch.step(dve.tensor_tensor(kT[:, :], kT[:, :], rT[:, :], add))
                dve.tensor_tensor_scan(wT[:, :], kT[:, :], kT[:, :], 0.0, add, ALU.max).then_inc(S.ranked, 1)
                dve.wait_ge(S.offset_ready, 2)
                ch.step(dve.tensor_copy(tot[:, 2:3], bank[4][:, 2:3]))
                dve.scalar_tensor_tensor(rT[:, :], wT[:, :], tot[:, 2:3], kT[:, :], add, mult).then_inc(S.slots_ready, 1)
                weight_scales(S, ch, 0)
                dve.wait_ge(S.back_turned, 1)
                dve.wait_ge(S.pstep, 3)
                vi, ai = t2[:, :, :].bitcast(i32), t3[:, :, :].bitcast(i32)
                ch.step(dve.tensor_scalar(vi.rearrange("p t e -> p (t e)"), bank[5][:, :], float(P - 1), None, add))
                ch.step(dve.tensor_scalar(ai, vi, P - 1, None, ALU.bitwise_and))
                ch.mark(dve.tensor_copy(pos_a[:, :, :].rearrange("p e t -> p t e"), ai))
                ch.step(dve.tensor_scalar(vi, vi, 7, None, ALU.logical_shift_right))
                ch.step(dve.tensor_copy(pos_b[:, :, :].rearrange("p e t -> p t e"), vi))

            def list_piece(S, n, i):
                r, at = i % 2, slice(i * LT, (i + 1) * LT)
                pa, pb = (col(a[:, :, at], n)[:, 0] for a in (pos_a, pos_b))
                dve.wait_ge(S.piece_used, LP * n + i + 1)
                dve.tensor_tensor(hot_b[:, r], bc(slot_b[:, :], 1, LT), bc(pb, 2, ST),
                                  ALU.is_equal).then_inc(S.hot_b_ready, 1)
                dve.tensor_tensor(hot_a[:, r], bc(pa, 1, P), slot_a[:, :, :], ALU.is_equal).then_inc(S.hot_a_ready, 1)

            def list_read(S, ch, n):
                dve.wait_ge(S.piece_used, LP * n + LP + 2)
                ch.step(dve.tensor_copy(lst[:, :], bank[6][:, 0:5 * ST]))
                ch.mark(dve.tensor_tensor(w_tmp[:, :], lst[:, 2 * ST:3 * ST], lst[:, 3 * ST:4 * ST], add))
                ch.wait()
                ch.mark(dve.tensor_tensor(w_next[:, :], w_tmp[:, :], lst[:, 4 * ST:5 * ST], add))
                dve.scalar_tensor_tensor(id_next[:, :], lst[:, 0:ST], float(P), lst[:, ST:2 * ST], mult,
                                         add).then_inc(S.ids_ready, 1)

            def unit(S, e, u):
                dve.wait_ge(S.u_ready, UNITS * e + u + 1)
                dve.wait_ge(S.s_ready, UNITS * e + u + 1 + 2)
                dve.wait_ge(S.h_ready, UNITS * e + u + 1)
                dve.scalar_tensor_tensor(h32[:, u % HB, :], bank[2 + u % 2][:, 0:CW], sc_cur[:, 4:5], act_s[:, u % 2, :],
                                         mult, mult).then_inc(S.h32_ready, 1)

            def unit_lo(S, e, u):
                f, c = divmod(u, CH)
                dve.wait_ge(S.hhi_ready, UNITS * e + u + 1)
                dve.tensor_tensor(hid[:, 1, f, c * CW:(c + 1) * CW], h32[:, u % HB, :],
                                  hid[:, 0, f, c * CW:(c + 1) * CW], sub).then_inc(S.h_ready, 1)

            def expert(S, ch, e, last):
                n = e + 1
                dve.wait_ge(S.scales_ready, e + 1)
                ch.mark(dve.tensor_copy(sc_cur[:, 2:3], sc_next[:, 2:3]))
                ch.mark(dve.tensor_scalar(sc_cur[:, 4:5], sc_next[:, 0:1], HSHIFT, None, mult))
                ch.mark(dve.tensor_scalar(sc_cur[:, 5:6], sc_next[:, 3:4], sc_next[:, 4:5], sc_next[:, 5:6], mult, mult))
                ch.wait()
                dve.tensor_scalar(sc_cur[:, 3:4], sc_next[:, 3:4], 1.0 / XSCALE, None, mult).then_inc(S.cur_ready, 1)
                for u in range(UNITS):
                    unit(S, e, u)
                    if u:
                        unit_lo(S, e, u - 1)
                    if u in (2, 4):
                        dve.wait_ge(S.d_hi, 2 * e + u // 2)
                        split_lo(2, u // 2 - 1, S.d_lo)
                    if u == 5:
                        dve.wait_ge(S.landed, e + 1)
                        ch.mark(dve.tensor_copy(id_cur[:, :], id_next[:, :]))
                        dve.tensor_scalar(w_fac[:, :], w_next[:, :], sc_cur[:, 5:6], 0.5 / (HSHIFT * XSCALE), mult,
                                          mult).then_inc(S.wfac_ready, 1)
                    if last:
                        continue
                    if u in AMAX_AT and not S.scaled:
                        m, i = AMAX_AT[u]
                        ch.mark(weight_amax(S, m, n, i))
                    if u in PIECE_AT:
                        list_piece(S, n, PIECE_AT[u])
                    if u == 26:
                        list_read(S, ch, n)
                unit_lo(S, e, UNITS - 1)
                if not last:
                    if not S.scaled:
                        ch.wait()
                        dve.tensor_reduce(am[:, :], am4[:, :, :], AX.X, ALU.max).then_inc(S.amax_ready, 1)
                    weight_scales(S, ch, n)
                    for k in range(4):
                        dve.wait_ge(S.gu_hi, 4 * n + k + 1)
                        split_lo(k % 2, k // 2, S.gu_lo)

            def ffn(S, wait_x, head, beside):
                ch = Chain(dve, S.dstep)
                ffn_in(S, ch, wait_x, head, beside)
                route(S, ch)
                for i in range(LP):
                    list_piece(S, 0, i)
                list_read(S, ch, 0)
                for k in range(4):
                    dve.wait_ge(S.gu_hi, k + 1)
                    split_lo(k % 2, k // 2, S.gu_lo)
                with dve.Fori(0, E - 1) as e:
                    ch.enter(e, 3 + 1 + 3 + (0 if S.scaled else 12 + 4))
                    expert(S, ch, e, False)
                    ch.leave(E - 1)
                expert(S, ch, E - 1, True)

            ch = Chain(dve, at.dstep)

            def attention_start():
                attention_constants()
                dve.wait_ge(s_atw, 16 * 4)
                for k in range(KD):
                    ch.mark(dve.tensor_scalar(mbv[:, k, :], same_h[:, :], bv_p[:, k:k + 1], None, mult))
                dve.wait_ge(at.a, 1)
                ch.step(dve.tensor_scalar(bvo[:, :, :].rearrange("p k d -> p (k d)"), bank[7][:, :], HS, None, mult))
                ch.mark(dve.scalar_tensor_tensor(bvo[:, :, :], bc(bo_b[:, :], 1, KD), 1.0 / (H * HS), bvo[:, :, :], mult, add))

            def stats(b, j):
                q, r = QUADS * b + j, j % 2
                if isinstance(b, int) and b == 0:
                    dve.wait_ge(x1_first, 16 * min(j + 1, 3))
                elif isinstance(b, int) and b == 1:
                    dve.wait_ge(at.x1_in, 16 * (j + 1))
                elif j == 0:
                    dve.wait_ge(at.x1_in, 16 * 2 * QUADS)
                wait_for(dve, at.xn, q - 1)
                for g in range(G4):
                    ch.mark(dve.bn_stats(bst[:, r, g, :], tiles(xs, G4 * q + g, 1)[:, 0]))
                ch.wait()
                settle(dve)
                for g in range(G4):
                    ch.mark(dve.bn_aggr(mv[:, r, g, :], bst[:, r, g, :]))
                ch.wait()
                dve.tensor_scalar(nmean[:, r, :], mv[:, r, :, 0], -1.0, None, mult)
                dve.tensor_scalar(rstd[:, r, :], mv[:, r, :, 1], EPS, XSCALE ** -2, add, mult).then_inc(at.stat, 1)

            def finish(b, j):
                q = QUADS * b + j
                for k in range(2):
                    dve.wait_ge(at.out, 2 * q + k + 1)
                    settle(dve)
                    x_k = tiles(xs, G4 * q + 2 * k, 2)
                    dve.scalar_tensor_tensor(x_k, bank[6 + k][:, :].rearrange("p (t d) -> p t d", t=2), mx2[:, 4:5],
                                             x_k, mult, add).then_inc(at.x2, 1)

            def by_head(ap):
                return ap.rearrange("p (h d) -> p h d", d=DH)

            def heads_of(j):
                return qb[:, j % 2].rearrange("p t (h d) -> p (t h) d", d=DH)

            def center(b, j):
                q, q3 = QUADS * b + j, heads_of(j)
                part = [slice(k * 2 * H, (k + 1) * 2 * H) for k in range(2)]
                for k in range(2):
                    dve.wait_ge(at.q, 2 * q + k + 1)
                    ch.mark(dve.tensor_reduce(qmax[:, part[k]], by_head(bank[2 + k][:, :]), AX.X, ALU.max))
                ch.wait()
                wait_for(dve, at.qlo, q - 1)
                for k in range(2):
                    i = dve.tensor_tensor(q3[:, part[k]], by_head(bank[2 + k][:, :]), bc(qmax[:, part[k]], 2, DH), sub)
                i.then_inc(at.cent, 1)

            def sum_heads(b, j):
                dve.wait_ge(at.ex, QUADS * b + j + 1)
                ch.step(dve.tensor_reduce(qsum, heads_of(j), AX.X, add))

            def soften(b, j):
                q3 = heads_of(j)
                ch.step(dve.reciprocal(qsum, qsum))
                dve.scalar_tensor_tensor(q3, q3, HS * QTOP, bc(qsum, 2, DH), mult, mult).then_inc(at.qs, 1)

            def m2_ctx(m):
                dve.wait_ge(at.ctx, m + 1)
                dve.tensor_tensor(ctm, bank[6][:, 0:KD * P].rearrange("p (k d) -> p k d", k=KD),
                                  bc(same_h[:, :], 1, KD), mult).then_inc(at.ctm, 1)

            def m2_out(m):
                dve.wait_ge(at.a, m + 2)
                for k in range(KD):
                    ch.mark(dve.scalar_tensor_tensor(m2f[:, k, :], bank[7][:, k * D:(k + 1) * D], zr[:, k:k + 1],
                                                     bvo[:, k, :], mult, add))
                ch.wait()
                dve.tensor_reduce(mx2[:, 0:1], m2f, AX.XY, ALU.max, apply_absolute_value=True).then_inc(at.m_amax, 1)

            def m2_scale(m):
                dve.wait_ge(at.m_max, m + 1)
                scales(ch, dve, mx2[:, 1:2], mx2[:, 2:3], mx2[:, 3:4])
                dve.tensor_scalar(mx2[:, 4:5], mx2[:, 3:4], 1.0 / QTOP, None, mult).then_inc(at.m_scale, 1)

            def m2_lo(m):
                dve.wait_ge(at.m_hi, m + 1)
                dve.scalar_tensor_tensor(m2h[:, 1], m2f, mx2[:, 2:3], m2h[:, 0], mult, sub).then_inc(at.m_lo, 1)

            def m2_sums(m):
                dve.wait_ge(at.gt, QUADS * (m + 1))
                ch.step(dve.reciprocal(zr[:, :], bank[5][:, 0:KD]))
                ch.mark(dve.tensor_scalar(zr[:, :], zr[:, :], HS, None, mult))

            def body(b, steps):
                for j in steps:
                    far, _, _, now, _, done = quads(b, j)
                    m = b - 1 if in_batches(b - 1) else None
                    if now:
                        center(*now)
                    if m is not None and j == 0:
                        m2_sums(m)
                        m2_ctx(m)
                        m2_out(m)
                    if far:
                        stats(*far)
                    if done and j == 1:
                        finish(done[0], 0)
                    if now:
                        sum_heads(*now)
                    if m is not None and j == 0:
                        m2_scale(m)
                    if now:
                        soften(*now)
                    if m is not None and j == 0:
                        m2_lo(m)
                    if done and j:
                        finish(*done)

            def looped(b, steps):
                if isinstance(b, int):
                    body(b, steps)
                else:
                    ch.enter(b - 1, LOOP_STEPS)
                    body(b, steps)
                    ch.leave(B - 2)

            def attention_end(n):
                if n == 1:
                    finish(B - 2, QUADS - 1)
                if n == 4:
                    m2_sums(B - 1)
                if n in (5, 7, 8, 9):
                    {5: m2_ctx, 7: m2_out, 8: m2_scale, 9: m2_lo}[n](B - 1)
                if n >= 14 and n % 2 == 0:
                    finish(B - 1, n // 2 - 7)

            def x_loaded(i, r):
                first = isinstance(i, int) and i == 0
                dve.wait_ge(sems[0].loaded, 16 * (r + 1 if first else i + 2))

            ffn(sems[0], x_loaded, 1, router)
            attention_start()
            batches(dve, looped)
            dve.wait_ge(at.lo, B * QUADS)
            ffn(sems[1], lambda i, r: dve.wait_ge(at.x2, 4 * i + 4 + 2), 5, attention_end)

        @block.tensor
        def _(pe):
            pe.wait_ge(s_gstep, 4)
            pe.wait_ge(s_boot, 6)
            for a in range(2):
                for k in range(KD):
                    o = (a * KD + k) * E
                    last = pe.transpose(bank16[7][:, o:o + E], rwh[:, a, k * P:(k + 1) * P], ident16[0:E, 0:E])
            last.then_inc(s_bootpe, 1)
            pe.wait_ge(s_boot, 7)
            HALVES = ((0, 0), (0, 1), (1, 0))

            def ffn_in(S, head, beside):
                def turn(q, r):
                    pe.wait_ge(S.lo_ready, q + 1 + 2)
                    for k in range(2):
                        pe.wait_ge(S.turned_ok, 2 * q + k + 1)
                        for t in range(2):
                            for c in range(2 * KD):
                                o = (t * 2 * KD + c) * P
                                i = pe.transpose(bank16[TURN_BANK[k]][:, o:o + P], rows[:, r, 2 * k + t, c * P:(c + 1) * P],
                                                 ident16[:, :])
                        i.then_inc(S.turned, 1)

                def logits(q, r):
                    for k in range(2):
                        pe.wait_ge(S.turned_ok, 2 * q + k + 1 + 2)
                        for t in range(2):
                            o = (r * G4 + 2 * k + t) * E
                            for j, (a, w) in enumerate(HALVES):
                                for d in range(KD):
                                    i = pe.matmul(bank[2][:, o:o + E], xt2[:, k, t, a * KD + d, :], rwT[:, w, d, :],
                                                  start=(j == 0 and d == 0), stop=(j == 2 and d == KD - 1))
                        i.then_inc(S.logit_ready, 1)

                def step(i, beside):
                    logits(2 * i - 1, 1)
                    turn(2 * i, 0)
                    beside(2 * i)
                    pe.wait_ge(S.logit_out, i + 1)
                    logits(2 * i, 0)
                    turn(2 * i + 1, 1)
                    beside(2 * i + 1)

                turn(0, 0)
                beside(0)
                logits(0, 0)
                beside(1)
                turn(1, 1)
                for i in range(1, 1 + head):
                    step(i, beside)
                with pe.Fori(1 + head, STEPS) as i:
                    step(i, nothing)
                logits(2 * STEPS - 1, 1)

            def route(S):
                pe.wait_ge(s_const, 1)
                pe.wait_ge(S.w_ready, 2)
                back = bank[5][:, :].rearrange("p (c g e) -> p g c e", g=G4, e=E)
                for g in range(G4):
                    last = pe.transpose(bank[3][:, g * P:(g + 1) * P], wT[:, g * P:(g + 1) * P], ident[:, :])
                last.then_inc(S.wt_turned, 1)
                with pe.Fori(0, ROUNDS) as r:
                    pe.wait_ge(S.compared, r + 1)
                    pe.wait_ge(S.third_counted, r + 1)
                    pe.matmul(bank[4][:, 0:3], same_e[:, :], cnt[:, 0:3], start=True, stop=True).then_inc(S.counted, 1)
                pe.wait_ge(S.ranked, 1)
                pe.matmul(bank[4][:, 0:1], same_e[:, :], cnt[:, 0:1], start=True, stop=True)
                pe.matmul(bank[4][:, 1:2], before_e[:, :], cnt[:, 1:2], start=True, stop=True).then_inc(S.offset_ready, 1)
                pe.wait_ge(S.ranked, 2)
                pe.matmul(bank[4][:, 2:3], before_e[:, :], wT[:, 4 * P - 1:4 * P], start=True,
                          stop=True).then_inc(S.offset_ready, 1)
                pe.wait_ge(S.slots_ready, 1)
                for g in range(G4):
                    last = pe.transpose(back[:, g], rT[:, g * P:(g + 1) * P], ident[:, :])
                last.then_inc(S.back_turned, 1)

            def list_piece(S, n, i):
                pe.wait_ge(S.hot_a_ready, LP * n + i + 1)
                pe.wait_ge(S.hot_v_ready, LP * n + i + 1)
                for t in range(LT):
                    last = pe.matmul(bank[6][:, 0:5 * ST], hot_a[:, i % 2, :, t],
                                     hot_v[:, i % 2, t].rearrange("p v s -> p (v s)"),
                                     start=(i == 0 and t == 0), stop=(i == LP - 1 and t == LT - 1))
                last.then_inc(S.piece_used, 1)

            def expert(S, e, last):
                n = e + 1
                for u in range(UNITS):
                    f, c = divmod(u, CH)
                    if u < CH:
                        for j in range(-(-u * CW // (2 * P)), -(-(u + 1) * CW // (2 * P))):
                            pe.wait_ge(turned[j], 32 * (e + S.first) + 32)
                    if u in (0, UNITS // 2):
                        pe.wait_ge(S.gu_lo, 4 * e + (2 if u == 0 else 4))
                    for m, (free, done) in enumerate(((S.s_ready, S.g_ready), (S.h32_ready, S.u_ready))):
                        pe.wait_ge(free, UNITS * e + u + 1)
                        for j, (a, w) in enumerate(HALVES):
                            for k in range(KD):
                                mm = pe.matmul(bank[2 * m + u % 2][:, 0:CW], wgu[m][:, w, k, f * P:(f + 1) * P],
                                               xT[:, a * KD + k, c * CW:(c + 1) * CW],
                                               start=(j == 0 and k == 0), stop=(j == 2 and k == KD - 1))
                        mm.then_inc(done, 1)
                    if not last and u in PE_PIECE_AT:
                        list_piece(S, n, PE_PIECE_AT[u])
                pe.wait_ge(S.d_lo, 2 * e + 2)
                for s in range(ST):
                    chunk = ((s + 1) * P - 1) // CW
                    pe.wait_ge(S.h_ready, UNITS * e + UNITS - CH + chunk + 1 + HB)
                    pe.wait_ge(S.d_out, ST * e + s + 1)
                    for f in range(FT):
                        for j, (a, w) in enumerate(HALVES):
                            mm = pe.matmul(bank[4 + s % 2][:, 0:D], hid[:, a, f, s * P:(s + 1) * P], wdn[:, w, f, :],
                                           start=(f == 0 and j == 0), stop=(f == FT - 1 and j == 2))
                    mm.then_inc(S.d_ready, 1)

            def ffn(S, head, beside):
                ffn_in(S, head, beside)
                route(S)
                for i in range(LP):
                    list_piece(S, 0, i)
                with pe.Fori(0, E - 1) as e:
                    expert(S, e, False)
                expert(S, E - 1, True)

            def attention_start():
                for k in range(KD):
                    if k == 0:
                        pe.wait_ge(at.dstep, KD)
                    i = pe.matmul(bank[7][:, k * D:(k + 1) * D], mbv[:, k, :], wo32[:, k, :], start=True, stop=True)
                i.then_inc(at.a, 1)

            def queries(b, j, k):
                q = QUADS * b + j
                wait_for(pe, at.cent, q)
                if k == 0:
                    pe.wait_ge(xt_in[j % 2], turned_by((b, j)))
                for t in range(2):
                    for n, (a, w) in enumerate(HALVES):
                        for d in range(KD):
                            i = pe.matmul(bank[2 + k][:, t * D:(t + 1) * D], at_xt[j % 2][:, 2 * k + t, a * KD + d, :],
                                          wq16[:, w, d, :], start=(n == 0 and d == 0), stop=False)
                    i = pe.matmul(bank[2 + k][:, t * D:(t + 1) * D], bq_one[:, :], bq16[:, :], start=False, stop=True)
                i.then_inc(at.q, 1)

            def keys(b, j):
                pe.wait_ge(at.eklo, QUADS * b + j + 1)
                for t in range(G4):
                    for m in range(KD):
                        for n, (a, w) in enumerate(HALVES):
                            pe.matmul(bank[4][:, m * D:(m + 1) * D], at_rows[j][:, t, a * D + m * P:a * D + (m + 1) * P],
                                      ekrow[:, j % 2, t, w * D:(w + 1) * D], start=(j == t == m == n == 0),
                                      stop=(j == QUADS - 1 and t == G4 - 1 and m == KD - 1 and n == 2))
                        for a in range(2):
                            i = pe.matmul(bank[5][:, m:m + 1], ekrow[:, j % 2, t, a * D + m * P:a * D + (m + 1) * P],
                                          ones[:, :], start=(j == t == m == a == 0),
                                          stop=(j == QUADS - 1 and t == G4 - 1 and m == KD - 1 and a == 1))
                i.then_inc(at.gt, 1)

            def finish(b, j):
                q = QUADS * b + j
                if j == 0:
                    pe.wait_ge(at.m_lo, b + 1)
                pe.wait_ge(qt_in[j % 2], turned_by((b, j)))
                for k in range(2):
                    if j:
                        pe.wait_ge(at.x2, 2 * q + k - 1 + 2)
                    for t in range(2):
                        for n, (a, w) in enumerate(HALVES):
                            for d in range(KD):
                                i = pe.matmul(bank[6 + k][:, t * D:(t + 1) * D], qT[:, G4 * j + 2 * k + t, a * KD + d, :],
                                              m2h[:, w, d, :], start=(n == 0 and d == 0), stop=(n == 2 and d == KD - 1))
                    i.then_inc(at.out, 1)

            def m2_ctx(m):
                pe.wait_ge(at.gt_out, m + 1)
                pe.wait_ge(at.x2, 2 * QUADS * m - 1 + 2)
                for n in range(KD):
                    for k in range(KD):
                        i = pe.matmul(bank[6][:, n * P:(n + 1) * P], wv32[:, k, n * P:(n + 1) * P],
                                      gt_s[:, k, n * P:(n + 1) * P], start=(k == 0), stop=(k == KD - 1))
                i.then_inc(at.ctx, 1)

            def m2_out(m):
                pe.wait_ge(at.ctm, m + 1)
                pe.wait_ge(at.x2, 2 * QUADS * m + 2)
                for k in range(KD):
                    i = pe.matmul(bank[7][:, k * D:(k + 1) * D], ctm[:, k, :], wo32[:, k, :], start=True, stop=True)
                i.then_inc(at.a, 1)

            def body(b, steps):
                for j in steps:
                    _, _, turned, _, past, done = quads(b, j)
                    if j == 0 and in_batches(b - 1):
                        m2_out(b - 1)
                    if done and j:
                        finish(done[0], j if j > 1 else 0)
                    if turned:
                        queries(*turned, 0)
                        queries(*turned, 1)
                    if done and j == 1:
                        finish(*done)
                    if past:
                        keys(*past)
                    if j == QUADS - 1 and in_batches(b):
                        m2_ctx(b)

            def attention_end(n):
                if n == -1:
                    finish(B - 2, QUADS - 1)
                    keys(B - 1, QUADS - 1)
                if n == 0:
                    m2_ctx(B - 1)
                if n == 1:
                    m2_out(B - 1)
                if n >= 4:
                    finish(B - 1, n - 4)

            ffn(sems[0], 0, nothing)
            attention_start()
            batches(pe, body)
            pe.wait_ge(at.cent, B * QUADS)
            attention_end(-1)
            ffn(sems[1], 3, attention_end)


_INS = ['L0_attn_x', 'L0_attn_Wq', 'L0_attn_bq', 'L0_attn_Wv', 'L0_attn_bv', 'L0_attn_Wo', 'L0_attn_bo',
        'L0_ffn_router_w', 'L0_ffn_wg', 'L0_ffn_wu', 'L0_ffn_wd']


def kernel(**inputs):
    import numpy as _np
    import concourse.bacc as _bacc
    from concourse import mybir as _mybir
    from concourse.bass_utils import run_bass_kernel_spmd as _run

    nc = _bacc.Bacc("TRN2", target_bir_lowering=False, num_devices=1)
    arrays, args = {}, []
    for name in _INS:
        a = _np.ascontiguousarray(inputs[name])
        arrays[f"in_{name}"] = a
        args.append(nc.dram_tensor(f"in_{name}", a.shape, _mybir.dt.from_np(a.dtype), kind="ExternalInput").ap())
    x = arrays["in_L0_attn_x"]
    out = nc.dram_tensor("out_x", x.shape, _mybir.dt.from_np(x.dtype), kind="ExternalOutput").ap()
    macaron_block(nc, *args, out)
    r = _run(nc, [arrays], core_ids=[0])
    return r.results[0]["out_x"]
```
